# Optimizing a Trainium2 kernel written in Bass

```python
import numpy as np
import jax
import jax.numpy as jnp

def _softmax(x, axis=-1):
    return jax.nn.softmax(x, axis=axis)

def _gelu(x):
    return jax.nn.gelu(x, approximate=True)

def _silu(x):
    return jax.nn.silu(x)

def _sigmoid(x):
    return jax.nn.sigmoid(x)

def _layernorm(x, axis=-1, eps=1e-05):
    m = jnp.mean(x, axis=axis, keepdims=True)
    v = jnp.var(x, axis=axis, keepdims=True)
    return (x - m) / jnp.sqrt(v + eps)

def _scatter_add(tgt, idx, src, axis=0):
    return tgt.at[idx].add(src)

def _segment_sum(src, seg, n):
    return jax.ops.segment_sum(src, seg, n)
kernel_name = 'mk_adj_resnorm_d1_adj_r2_8a946d'

def setup_inputs(seed: int=0):
    np.random.seed(seed)
    _w = jnp.asarray

    def _rec_inputs():
        import jax
        import jax.numpy as jnp
        _gk = jax.random.key(seed)
        x = -9.806e-05 + 1 * jax.random.normal(jax.random.fold_in(_gk, 1), (4096, 64), jnp.float32)
        _a = jax.random.bernoulli(jax.random.fold_in(_gk, 2), 0.00195312, (4096, 4096))
        adj = _a.astype(jnp.int32)
        return (x, adj)
    x, adj = _rec_inputs()

    def _L0_gnn_setup():
        import jax, jax.numpy as jnp
        import numpy as np
        N = 4096
        D = 64
        NEG_INF = -9000000000000000.0
        LEAKY_SLOPE = 0.01
        key = jax.random.key(seed)
        k1, k2, k3 = jax.random.split(key, 3)
        h = jax.random.normal(k1, (N, D), dtype=jnp.float32)
        adj = jax.random.randint(k2, (N, N), 0, 2, dtype=jnp.int32)
        bound = float(np.sqrt(6.0 / (2 * D + 1)))
        a = jax.random.uniform(k3, (2 * D, 1), dtype=jnp.float32, minval=-bound, maxval=bound)
        return {'h': h, 'adj': adj, 'a': a}
    _L0_gnn_all = _L0_gnn_setup()
    _L0_gnn_in = {k: v for k, v in _L0_gnn_all.items() if k in ('a',)}
    del _L0_gnn_all
    return {'x': x, 'adj': adj, 'L0_gnn_a': _L0_gnn_in['a']}

def reference(x, adj, L0_gnn_a):
    import jax
    import jax.numpy as jnp

    def _L0_gnn_ref(h, adj, a):
        import jax, jax.numpy as jnp
        import numpy as np
        N = 4096
        D = 64
        NEG_INF = -9000000000000000.0
        LEAKY_SLOPE = 0.01
        a1 = a[:D, 0]
        a2 = a[D:, 0]
        src = h @ a1
        dst = h @ a2
        e = src[:, None] + dst[None, :]
        e = jnp.where(e > 0, e, LEAKY_SLOPE * e)
        e = jnp.where(adj > 0, e, NEG_INF)
        attention = jax.nn.softmax(e, axis=1)
        h_prime = attention @ h
        return h_prime
    x = _layernorm(x + _L0_gnn_ref(x, adj, L0_gnn_a), axis=-1)
    return x

_drawn_inputs = setup_inputs


def setup_inputs(seed=0):
    import zlib

    import numpy as np

    out = dict(_drawn_inputs(seed))
    spreads = {}
    factors = {}
    for name, (base, spread) in spreads.items():
        noise = np.random.default_rng([zlib.crc32(name.encode()), seed]).standard_normal(out[name].shape)
        drawn = base * np.exp(spread * noise) if base else spread * noise
        out[name] = jnp.asarray(drawn.astype(out[name].dtype))
    for name, factor in factors.items():
        out[name] = (out[name] * factor).astype(out[name].dtype)
    return out
```

```python
from contextlib import ExitStack

import concourse.bass as bass
from concourse import mybir
import numpy as np

ALU = mybir.AluOpType
ACT = mybir.ActivationFunctionType
AX_X = mybir.AxisListType.X
F32 = mybir.dt.float32
F16 = mybir.dt.float16
BF16 = mybir.dt.bfloat16
FP8 = mybir.dt.float8e4
I32 = mybir.dt.int32
RMAX = bass.bass_isa.ReduceOp.max

P = 128
SLOPE = 0.01
NEG_INF = -9000000000000000.0
EPS = 1e-5

ABOVE = 1.0
ABOVE_BYTE = 1.875
BELOW = float(np.array([0x00B80000], np.uint32).view(np.float32)[0])
BELOW_BYTE = -1.0

G_SCALE = 2048.0
MAX_SPREAD = 9.0
MIN_X, MAX_X = 0.5, 16.0


def gat_layernorm(nc, x, adj, a, out):
    N, D = x.shape
    NB = N // P
    T = 4
    CR = T * P
    C = N // CR
    SLABS = 4
    SW = N // SLABS
    PAIR = 2
    GROUPS = NB // PAIR
    GPS = GROUPS // SLABS
    LAG = 2
    W = D + 1
    RB = 4
    COPY_AT = LAG - 1
    ROT = 13

    x_j = x.rearrange("(b p) d -> p b d", p=P)
    x_i = x.rearrange("(c p t) d -> p c (t d)", p=P, t=T)
    adj_i = adj.rearrange("(c p t) j -> c p t j", p=P, t=T)
    out_i = out.rearrange("(c p t) d -> c p (t d)", p=P, t=T)
    adj_k = adj.rearrange("(k p) j -> k p j", p=P)
    x_k = x.rearrange("(k p) d -> k p d", p=P)
    out_k = out.rearrange("(k p) d -> k p d", p=P)
    a_row = a.rearrange("(a n) o -> o a n", a=2)
    a_col = a.rearrange("(a n) o -> n (a o)", a=2)

    with ExitStack() as ctx:
        def sb(name, shape, dt):
            return ctx.enter_context(nc.sbuf_tensor(name, shape, dt))

        def pb(name, shape, dt):
            return ctx.enter_context(nc.psum_tensor(name, shape, dt))

        def sem(name):
            return ctx.enter_context(nc.semaphore(name))

        ring = sb("ring", [P, SLABS, T, SW], I32)
        ident = sb("ident", [P, P], F32)
        ones = sb("ones", [P, P], F32)
        xj = sb("xj", [P, NB, W], F32)
        xi = sb("xi", [P, C, T * D], F32)
        xt = sb("xt", [D, N], F32)
        a_rows = sb("a_rows", [P, 2, D], F32)
        a_cols = sb("a_cols", [D, 2], F32)
        a_rep = sb("a_rep", [D, 2, P], F32)
        d = sb("d", [P, NB], F32)
        s = sb("s", [P, NB], F32)
        nd = sb("nd", [P, NB], F32)
        stats = sb("stats", [P, 3], F32)
        top = sb("top", [P, 3], F32)
        bias = sb("bias", [P, 2], F32)
        spread = sb("spread", [P, 4], F32)
        flag = sb("flag", [P, 1], I32)
        e12 = sb("e12", [P, 2, NB], F32)
        u = sb("u", [P, 3, NB], F32)
        ff = sb("ff", [P, NB, 2], F32)
        g32 = sb("g32", [P, 2, NB, W], F32)
        g = sb("g", [P, 2, NB, 2, W], F16)
        tree = sb("tree", [P, NB // 2, W], F32)
        mean_row = sb("mean_row", [P, W], F32)
        s_all = sb("s_all", [P, C, CR], F32)
        thr = sb("thr", [P, RB, PAIR, CR], BF16)
        clean = sb("clean", [P, RB, PAIR, CR], BF16)
        code = sb("code", [P, RB, PAIR, CR], BF16)
        prod = code[:, :, :, :].rearrange("p r b i -> p (r b i)").bitcast(F32).rearrange("p (b d) -> p b d", d=D)
        prod_i = clean[:, :, :, :].rearrange("p r b i -> p (r b i)").bitcast(F32).rearrange("p (b d) -> p b d", d=D)
        sums = sb("sums", [P, T, 2, 2, W], F32)
        scaled = sb("scaled", [P, T, 2, 2, W], F32)
        planes = sb("planes", [P, T, 2, W], F32)
        total = sb("total", [P, T, W], F32)
        empty = sb("empty", [P, T], F32)
        fill = sb("fill", [P, T, D], F32)
        full = sb("full", [P, T, D], F32)
        rden = sb("rden", [P, T], F32)
        att = sb("att", [P, T, D], F32)
        z = sb("z", [P, T, D], F32)
        zsum = sb("zsum", [P, T], F32)
        mean = sb("mean", [P, T], F32)
        zc = sb("zc", [P, T, D], F32)
        sq = sb("sq", [P, T, D], F32)
        vsum = sb("vsum", [P, T], F32)
        den = sb("den", [P, T], F32)
        eps = sb("eps", [P, 1], F32)
        inv_d = sb("inv_d", [P, T], F32)
        dev = sb("dev", [P, T], F32)
        rstd = sb("rstd", [P, T], F32)
        res = sb("res", [P, T, D], F32)
        gadj = ring[:, 0, :, :].rearrange("p t w -> p (t w)")
        gd = ring[:, 1, :, :].rearrange("p t w -> p (t w)").bitcast(F32)
        ge = ring[:, 2, :, :].rearrange("p t w -> p (t w)").bitcast(F32)
        gt = ring[:, 3, :, :].rearrange("p t w -> p (t w)").bitcast(F32)
        gx = sb("gx", [P, D], F32)
        gv = sb("gv", [P, 10], F32)
        gy = sb("gy", [P, 4, D], F32)

        pt = pb("pt", [P, 2, PAIR * CR], F32)
        acc = pb("acc", [P, T, 512], F32)

        xj_loaded = [sem(f"xj_loaded{q}") for q in range(4)]
        xi_loaded = sem("xi_loaded")
        a_loaded = sem("a_loaded")
        slab_loaded = [sem(f"slab_loaded{k}") for k in range(SLABS)]
        group_transposed = sem("group_transposed")
        mask_clean = sem("mask_clean")
        thr_ready = sem("thr_ready")
        code_ready = sem("code_ready")
        products_done = sem("products_done")
        sums_copied = sem("sums_copied")
        consts_ready = sem("consts_ready")
        ones_ready = sem("ones_ready")
        x_transposed = sem("x_transposed")
        xt_copied = sem("xt_copied")
        a_rep_ready = sem("a_rep_ready")
        s_summed = sem("s_summed")
        s_copied = sem("s_copied")
        dot_d = sem("dot_d")
        nd_ready = sem("nd_ready")
        stats_ready = sem("stats_ready")
        top_ready = sem("top_ready")
        bias_ready = sem("bias_ready")
        e_ready = sem("e_ready")
        e_scaled = sem("e_scaled")
        g32_ready = sem("g32_ready")
        ghi_ready = sem("ghi_ready")
        g_ready = sem("g_ready")
        flag_step = sem("flag_step")
        flag_ready = sem("flag_ready")
        prod_i_ready = sem("prod_i_ready")
        s_ready = sem("s_ready")
        u_step = sem("u_step")
        u_ready = sem("u_ready")
        f_ready = sem("f_ready")
        ff_ready = sem("ff_ready")
        tree_step = sem("tree_step")
        tree_ready = sem("tree_ready")
        mean_summed = sem("mean_summed")
        pool_step = sem("pool_step")
        den_ready = sem("den_ready")
        rden_ready = sem("rden_ready")
        z_ready = sem("z_ready")
        zsum_ready = sem("zsum_ready")
        sq_ready = sem("sq_ready")
        vsum_ready = sem("vsum_ready")
        dev_ready = sem("dev_ready")
        rstd_ready = sem("rstd_ready")
        res_ready = sem("res_ready")
        res_stored = sem("res_stored")
        sums_scaled = sem("sums_scaled")
        total_ready = sem("total_ready")
        gen_d = sem("gen_d")
        gen_d_copied = sem("gen_d_copied")
        gen_loaded = sem("gen_loaded")
        gen_step = sem("gen_step")
        gen_masked = sem("gen_masked")
        gen_weights = sem("gen_weights")
        gen_turned = sem("gen_turned")
        gen_copied = sem("gen_copied")
        gen_summed = sem("gen_summed")
        gen_var = sem("gen_var")
        gen_dev = sem("gen_dev")
        gen_res = sem("gen_res")
        gen_stored = sem("gen_stored")

        block = ctx.enter_context(nc.Block())

        def general(eng):
            eng.wait_ge(flag_ready, 1)
            return eng.If(eng.value_load(flag[0:1, 0:1], min_val=0, max_val=1) > 0)

        @block.sync
        def _(sp):
            for q in range(4):
                bq = NB // 4
                sp.dma_start(xj[:, q * bq:(q + 1) * bq, 0:D], x_j[:, q * bq:(q + 1) * bq, :]).then_inc(xj_loaded[q], 16)

            def load(c, k):
                sp.dma_start(ring[:, k, :, :], adj_i[c, :, :, k * SW:(k + 1) * SW]).then_inc(slab_loaded[k], 16)

            for k in range(SLABS):
                load(0, k)
            with sp.Fori(1, C) as c:
                for k in range(SLABS):
                    sp.wait_ge(group_transposed, c * GROUPS + ((k + 1) * GPS - GROUPS))
                    load(c, k)
            with general(sp):
                sp.wait_ge(group_transposed, C * GROUPS)
                sp.wait_ge(res_stored, C * 16)

                def load_tile(k):
                    sp.dma_start(gadj, adj_k[k]).then_inc(gen_loaded, 16)
                    sp.dma_start(gx[:, :], x_k[k]).then_inc(gen_loaded, 16)

                def store_tile(k):
                    sp.wait_ge(gen_res, k + 1)
                    sp.dma_start(out_k[k], gy[:, 3, :]).then_inc(gen_stored, 16)
                    sp.wait_ge(gen_stored, (k + 1) * 16)

                load_tile(0)
                with sp.Fori(0, NB - 1) as k:
                    store_tile(k)
                    load_tile(k + 1)
                store_tile(NB - 1)

        @block.tensor
        def _(pe):
            def transposes(c, gr, then=None):
                n = c * GROUPS + gr
                k, col = gr // GPS, (gr % GPS) * PAIR * P
                if gr % GPS == 0:
                    pe.wait_ge(slab_loaded[k], (c + 1) * 16)
                if not (isinstance(n, int) and n < 2):
                    pe.wait_ge(mask_clean, n - 1)
                for b in range(PAIR):
                    for t in range(T):
                        if then and b == PAIR - 1 and t == T - 1:
                            products_wait(*then)
                        last = nc.tensor.transpose(pt[:, gr % 2, b * CR + t * P:b * CR + (t + 1) * P],
                                                   ring[:, k, t, col + b * P:col + (b + 1) * P].bitcast(F32),
                                                   ident[:, :])
                last.then_inc(group_transposed, 1)

            def products_wait(c, gr):
                pe.wait_ge(code_ready, c * GROUPS + gr + 1)
                if gr == 0:
                    pe.wait_ge(sums_copied, c + 1)

            def products(c, gr):
                for b in range(PAIR):
                    blk = gr * PAIR + b
                    for t in range(T):
                        both = code[:, gr % RB, b, t * P:(t + 1) * P].bitcast(FP8).rearrange("p (i h) -> p h i", h=2)
                        nc.tensor.matmul(acc[:, t, 0:2 * W], both[:, 1, :],
                                         g[:, 0, blk, :, :].rearrange("p h w -> p (h w)"),
                                         start=(blk == 0), stop=(blk == NB - 1), skip_group_check=True)
                        last = nc.tensor.matmul(acc[:, t, 2 * W:4 * W], both[:, 0, :],
                                                g[:, 1, blk, :, :].rearrange("p h w -> p (h w)"),
                                                start=False, stop=(blk == NB - 1), skip_group_check=True)
                last.then_inc(products_done, 1)

            pe.wait_ge(consts_ready, 5)
            for q in range(4):
                pe.wait_ge(xj_loaded[q], 16)
                for h in range(2):
                    for m in range(4):
                        b = q * 8 + h * 4 + m
                        bank = acc[0:D, q, m * P:(m + 1) * P] if h == 0 else \
                            pt[0:D, q // 2, (q % 2) * 512 + m * P:(q % 2) * 512 + (m + 1) * P]
                        last = nc.tensor.transpose(bank, xj[:, b, 0:D], ident[:, :])
                    last.then_inc(x_transposed, 1)
            pe.wait_ge(a_rep_ready, 1)
            for c in range(C):
                pe.wait_ge(xt_copied, c + 1)
                bank = acc[:, c // 2, :] if c % 2 == 0 else pt[:, c // 4, (c // 2 % 2) * 512:(c // 2 % 2 + 1) * 512]
                nc.tensor.matmul(bank, a_rep[:, 0, :],
                                 xt[:, c * CR:(c + 1) * CR].rearrange("n (p t) -> n t p", t=T),
                                 start=True, stop=True).then_inc(s_summed, 1)
            pe.wait_ge(tree_ready, 1)
            pe.wait_ge(s_copied, 1)
            nc.tensor.matmul(acc[:, 0, 0:W], ones[:, :], tree[:, 0, :], start=True, stop=True).then_inc(mean_summed, 1)
            pe.wait_ge(s_copied, C)
            for gr in range(LAG):
                transposes(0, gr)
            pe.wait_ge(g_ready, 2)

            def chunk(c, more):
                for gr in range(GROUPS):
                    if gr + LAG < GROUPS:
                        transposes(c, gr + LAG, (c, gr))
                    elif more:
                        transposes(c + 1, gr + LAG - GROUPS, (c, gr))
                    else:
                        products_wait(c, gr)
                    products(c, gr)

            with pe.Fori(0, C - 1) as c:
                chunk(c, True)
            chunk(C - 1, False)

            with general(pe):
                pe.wait_ge(sums_copied, C + 1)
                for q in range(8):
                    if q >= 1:
                        pe.wait_ge(gen_d_copied, q)
                    nc.tensor.matmul(acc[:, 0, :], a_rep[:, 1, :], xt[:, q * 512:(q + 1) * 512],
                                     start=True, stop=True).then_inc(gen_d, 1)
                pe.wait_ge(gen_d_copied, 8)
                with pe.Fori(0, NB) as k:
                    pe.wait_ge(gen_weights, k + 1)
                    for h in range(2):
                        if h == 1:
                            pe.wait_ge(gen_copied, k * 2 + 1)
                        for m in range(16):
                            last = nc.tensor.transpose(pt[:, m // 8, (m % 8) * P:(m % 8 + 1) * P],
                                                       ge[:, (h * 16 + m) * P:(h * 16 + m + 1) * P], ident[:, :])
                        last.then_inc(gen_turned, 1)
                    pe.wait_ge(gen_copied, k * 2 + 2)
                    for b in range(NB):
                        last = nc.tensor.matmul(acc[:, 0, 0:D], gt[:, b * P:(b + 1) * P], xj[:, b, 0:D],
                                                start=(b == 0), stop=(b == NB - 1))
                    last.then_inc(gen_summed, 1)

        @block.scalar
        def _(act):
            with nc.allow_non_contiguous_dma(reason="256 bytes of a"):
                act.dma_start(a_cols[:, :], a_col).then_inc(a_loaded, 16)
            act.dma_start(a_rows[:, :, :], a_row.to_broadcast([P, 2, D])).then_inc(a_loaded, 16)
            act.dma_start(xi[:, :, :], x_i).then_inc(xi_loaded, 16)

            for c in range(C):
                act.wait_ge(x_transposed, c + 1)
                bank = acc[0:D, c // 2, :] if c % 2 == 0 else \
                    pt[0:D, c // 4, (c // 2 % 2) * 512:(c // 2 % 2 + 1) * 512]
                nc.scalar.copy(xt[:, c * CR:(c + 1) * CR], bank).then_inc(xt_copied, 1)
            act.wait_ge(bias_ready, 2)
            nc.scalar.activation(e12[:, 0, :], d[:, :], ACT.Exp, bias=bias[:, 0:1], scale=1.0).then_inc(e_ready, 1)
            nc.scalar.activation(e12[:, 1, :], d[:, :], ACT.Exp, bias=bias[:, 1:2], scale=SLOPE).then_inc(e_ready, 1)
            for c in range(C):
                act.wait_ge(s_summed, c + 1)
                bank = acc[:, c // 2, :] if c % 2 == 0 else pt[:, c // 4, (c // 2 % 2) * 512:(c // 2 % 2 + 1) * 512]
                nc.scalar.copy(s_all[:, c, :], bank).then_inc(s_copied, 1)
            for w in range(2):
                act.wait_ge(g32_ready, w + 1)
                nc.scalar.copy(g[:, w, :, 0, :], g32[:, w, :, :]).then_inc(ghi_ready, 1)
            act.wait_ge(mean_summed, 1)
            nc.scalar.copy(mean_row[:, :], acc[:, 0, 0:W]).then_inc(sums_copied, 1)
            act.wait_ge(u_ready, 2)
            nc.scalar.activation(u[:, 0, :], u[:, 1, :], ACT.Exp, scale=1.0 - SLOPE).then_inc(f_ready, 1)
            act.wait_ge(f_ready, 1)
            nc.scalar.mul(ff[:, :, 0], u[:, 0, :], 1.0 / ABOVE_BYTE).then_inc(ff_ready, 1)
            nc.scalar.activation(u[:, 1, :], u[:, 2, :], ACT.Exp, scale=SLOPE - 1.0).then_inc(f_ready, 1)
            act.wait_ge(f_ready, 2)
            nc.scalar.mul(ff[:, :, 1], u[:, 1, :], 1.0 / BELOW_BYTE).then_inc(ff_ready, 1)

            def clean_mask(c, gr):
                n = c * GROUPS + gr
                act.wait_ge(group_transposed, n + 1)
                if not (isinstance(n, int) and n < RB):
                    act.wait_ge(code_ready, n + (1 - RB))
                nc.scalar.activation(clean[:, gr % RB, :, :].rearrange("p b i -> p (b i)"),
                                     pt[:, gr % 2, :].bitcast(I32), ACT.Relu).then_inc(mask_clean, 1)

            def copy_sums(c):
                act.wait_ge(products_done, (c + 1) * GROUPS)
                act.wait_ge(sums_scaled, c + 1)
                nc.scalar.copy(sums[:, :, :, :, :].rearrange("p t a h w -> p t (a h w)"),
                               acc[:, :, 0:4 * W]).then_inc(sums_copied, 1)

            def deviation(c):
                act.wait_ge(vsum_ready, c + 1)
                nc.scalar.activation(dev[:, :], vsum[:, :], ACT.Sqrt, bias=eps[:, :], scale=1.0 / D)\
                    .then_inc(dev_ready, 1)

            for gr in range(ROT):
                clean_mask(0, gr)
            with act.Fori(0, C - 1) as c:
                for gr in range(ROT, GROUPS):
                    clean_mask(c, gr)
                for gr in range(ROT):
                    clean_mask(c + 1, gr)
                    if gr == COPY_AT:
                        copy_sums(c)
                    if gr == ROT - 1:
                        deviation(c)
            for gr in range(ROT, GROUPS):
                clean_mask(C - 1, gr)
            copy_sums(C - 1)
            deviation(C - 1)

            with general(act):
                with act.Fori(0, NB) as k:
                    act.wait_ge(gen_masked, k + 1)
                    nc.scalar.activation(ge, ge, ACT.Exp, bias=gv[:, 2:3], scale=1.0,
                                         accum_out=gv[:, 3:4]).then_inc(gen_weights, 1)
                    act.wait_ge(gen_var, k + 1)
                    nc.scalar.activation(gv[:, 8:9], gv[:, 7:8], ACT.Sqrt).then_inc(gen_dev, 1)

        @block.vector
        def _(dve):
            def threshold(c, gr):
                n = c * GROUPS + gr
                if not (isinstance(n, int) and n < RB):
                    dve.wait_ge(code_ready, n + (1 - RB))
                for b in range(PAIR):
                    blk = gr * PAIR + b
                    nc.vector.tensor_scalar(thr[:, gr % RB, b, :], s_all[:, c, :], nd[:, blk:blk + 1], BELOW,
                                            ALU.is_gt, ALU.max).then_inc(thr_ready, 1)

            def select(c, gr):
                n = c * GROUPS + gr
                dve.wait_ge(thr_ready, (n + 1) * PAIR)
                dve.wait_ge(mask_clean, n + 1)
                if not (isinstance(n, int) and n < RB):
                    dve.wait_ge(products_done, n + (1 - RB))
                nc.vector.tensor_tensor(code[:, gr % RB, :, :], clean[:, gr % RB, :, :], thr[:, gr % RB, :, :],
                                        ALU.min).then_inc(code_ready, 1)

            dve.wait_ge(consts_ready, 5)
            dve.wait_ge(a_loaded, 32)
            for w in range(2):
                last = nc.vector.tensor_copy(a_rep[:, w, :], a_cols[:, w:w + 1].to_broadcast([D, P]))
            last.then_inc(a_rep_ready, 1)
            for q in range(4):
                dve.wait_ge(xj_loaded[q], 16)
            nc.vector.tensor_tensor(prod[:, :, :], xj[:, :, 0:D],
                                    a_rows[:, 1:2, :].to_broadcast([P, NB, D]), ALU.mult).then_inc(dot_d, 1)
            nc.vector.tensor_reduce(stats[:, 2:3], xj[:, :, 0:D], mybir.AxisListType.XY, ALU.max,
                                    apply_absolute_value=True)
            dve.wait_ge(dot_d, 1)
            nc.vector.tensor_reduce(d[:, :], prod[:, :, :], AX_X, ALU.add).then_inc(dot_d, 1)
            dve.wait_ge(dot_d, 2)
            nc.vector.tensor_scalar(nd[:, :], d[:, :], -1.0, None, ALU.mult).then_inc(nd_ready, 1)
            nc.vector.tensor_reduce(stats[:, 0:1], d[:, :], AX_X, ALU.max)
            dve.wait_ge(nd_ready, 1)
            nc.vector.tensor_reduce(stats[:, 1:2], nd[:, :], AX_X, ALU.max).then_inc(stats_ready, 1)
            dve.wait_ge(top_ready, 1)
            nc.vector.tensor_scalar(bias[:, 0:1], top[:, 0:1], -1.0, None, ALU.mult).then_inc(bias_ready, 1)
            nc.vector.tensor_scalar(bias[:, 1:2], top[:, 0:1], -SLOPE, None, ALU.mult).then_inc(bias_ready, 1)
            dve.wait_ge(e_ready, 2)
            nc.vector.tensor_scalar(e12[:, :, :], e12[:, :, :], G_SCALE, None, ALU.mult).then_inc(e_scaled, 1)
            dve.wait_ge(e_scaled, 1)
            for w in range(2):
                nc.vector.tensor_tensor(g32[:, w, :, :], xj[:, :, :],
                                        e12[:, w, :].unsqueeze(2).to_broadcast([P, NB, W]),
                                        ALU.mult).then_inc(g32_ready, 1)
            for w in range(2):
                dve.wait_ge(ghi_ready, w + 1)
                nc.vector.tensor_tensor(g[:, w, :, 1, :], g32[:, w, :, :], g[:, w, :, 0, :],
                                        ALU.subtract).then_inc(g_ready, 1)
            dve.wait_ge(prod_i_ready, 1)
            nc.vector.tensor_reduce(s[:, :], prod_i[:, :, :], AX_X, ALU.add).then_inc(s_ready, 1)
            dve.wait_ge(s_ready, 1)
            nc.vector.tensor_scalar(u[:, 0, :], s[:, :], top[:, 0:1], None, ALU.add).then_inc(u_step, 1)
            dve.wait_ge(u_step, 1)
            nc.vector.tensor_scalar(u[:, 1, :], u[:, 0, :], 0.0, None, ALU.min).then_inc(u_ready, 1)
            nc.vector.tensor_scalar(u[:, 2, :], u[:, 0, :], 0.0, None, ALU.max).then_inc(u_ready, 1)
            nc.vector.tensor_scalar(spread[:, 0:1], top[:, 0:1], top[:, 1:2], MAX_SPREAD, ALU.add,
                                    ALU.is_le).then_inc(flag_step, 1)
            nc.vector.tensor_scalar(spread[:, 1:2], top[:, 2:3], MIN_X, None, ALU.is_ge).then_inc(flag_step, 1)
            dve.wait_ge(flag_step, 2)
            nc.vector.scalar_tensor_tensor(out=spread[:, 2:3], in0=top[:, 2:3], scalar=MAX_X, in1=spread[:, 1:2],
                                           op0=ALU.is_le, op1=ALU.mult).then_inc(flag_step, 1)
            dve.wait_ge(flag_step, 3)
            nc.vector.tensor_tensor(spread[:, 3:4], spread[:, 0:1], spread[:, 2:3], ALU.mult).then_inc(flag_step, 1)
            dve.wait_ge(flag_step, 4)
            nc.vector.tensor_scalar(flag[:, :], spread[:, 3:4], -1.0, 1.0, ALU.mult, ALU.add).then_inc(flag_ready, 1)

            def recip_den(c):
                dve.wait_ge(total_ready, c + 1)
                nc.vector.tensor_scalar(empty[:, :], total[:, :, D], 0.0, None, ALU.is_equal).then_inc(den_ready, 1)
                dve.wait_ge(den_ready, c * 2 + 1)
                nc.vector.scalar_tensor_tensor(out=den[:, :], in0=empty[:, :], scalar=float(N), in1=total[:, :, D],
                                               op0=ALU.mult, op1=ALU.add).then_inc(den_ready, 1)
                dve.wait_ge(den_ready, c * 2 + 2)
                nc.vector.reciprocal(rden[:, :], den[:, :]).then_inc(rden_ready, 1)

            def sum_z(c):
                dve.wait_ge(z_ready, c + 1)
                nc.vector.tensor_reduce(zsum[:, :], z[:, :, :], AX_X, ALU.add).then_inc(zsum_ready, 1)

            def sum_sq(c):
                dve.wait_ge(sq_ready, c + 1)
                nc.vector.tensor_reduce(vsum[:, :], sq[:, :, :], AX_X, ALU.add).then_inc(vsum_ready, 1)

            def recip_dev(c):
                dve.wait_ge(dev_ready, c + 1)
                nc.vector.reciprocal(rstd[:, :], dev[:, :]).then_inc(rstd_ready, 1)

            dve.wait_ge(s_copied, 1)
            threshold(0, 0)
            for gr in range(ROT):
                if gr == 0:
                    dve.wait_ge(s_copied, C)
                threshold(0, gr + 1)
                select(0, gr)
            with dve.Fori(0, C - 1) as c:
                for gr in range(ROT, GROUPS):
                    threshold(c, gr + 1) if gr + 1 < GROUPS else threshold(c + 1, 0)
                    select(c, gr)
                for gr in range(ROT):
                    if gr == 5:
                        recip_den(c)
                    if gr == 7:
                        sum_z(c)
                    if gr == 9:
                        sum_sq(c)
                    threshold(c + 1, gr + 1)
                    select(c + 1, gr)
                recip_dev(c)
            for gr in range(ROT, GROUPS):
                if gr + 1 < GROUPS:
                    threshold(C - 1, gr + 1)
                select(C - 1, gr)
            recip_den(C - 1)
            sum_z(C - 1)
            sum_sq(C - 1)
            recip_dev(C - 1)

            with general(dve):
                chain = [0]
                for q in range(8):
                    dve.wait_ge(gen_d, q + 1)
                    nc.vector.tensor_copy(gd[:, q * 512:(q + 1) * 512], acc[:, 0, :]).then_inc(gen_d_copied, 1)
                dve.wait_ge(gen_d_copied, 8)
                STEPS = 16
                with dve.Fori(0, NB) as k:
                    def link(ins):
                        chain[0] += 1
                        ins.then_inc(gen_step, 1)
                        dve.wait_ge(gen_step, k * STEPS + chain[0])

                    dve.wait_ge(gen_loaded, (k + 1) * 32)
                    link(nc.vector.tensor_tensor(gy[:, 0, :], gx[:, :], a_rows[:, 0, :], ALU.mult))
                    link(nc.vector.tensor_reduce(gv[:, 0:1], gy[:, 0, :], AX_X, ALU.add))
                    link(nc.vector.tensor_scalar(gt, gd, gv[:, 0:1], None, ALU.add))
                    link(nc.vector.scalar_tensor_tensor(out=ge, in0=gt, scalar=SLOPE, in1=gt,
                                                        op0=ALU.mult, op1=ALU.max))
                    link(nc.vector.scalar_tensor_tensor(out=gt, in0=gadj, scalar=0.0, in1=ge,
                                                        op0=ALU.is_gt, op1=ALU.mult))
                    link(nc.vector.tensor_scalar(ge, gadj, 0.0, -1.0, ALU.is_gt, ALU.add))
                    link(nc.vector.scalar_tensor_tensor(out=ge, in0=ge, scalar=-NEG_INF, in1=gt,
                                                        op0=ALU.mult, op1=ALU.add))
                    link(nc.vector.tensor_reduce(gv[:, 1:2], ge, AX_X, ALU.max))
                    nc.vector.tensor_scalar(gv[:, 2:3], gv[:, 1:2], -1.0, None, ALU.mult).then_inc(gen_masked, 1)
                    for h in range(2):
                        dve.wait_ge(gen_turned, k * 2 + h + 1)
                        nc.vector.tensor_copy(gt[:, h * 2048:(h + 1) * 2048],
                                              pt[:, :, :].rearrange("p a w -> p (a w)")).then_inc(gen_copied, 1)
                    dve.wait_ge(gen_summed, k + 1)
                    link(nc.vector.reciprocal(gv[:, 4:5], gv[:, 3:4]))
                    link(nc.vector.scalar_tensor_tensor(out=gy[:, 1, :], in0=acc[:, 0, 0:D], scalar=gv[:, 4:5],
                                                        in1=gx[:, :], op0=ALU.mult, op1=ALU.add))
                    link(nc.vector.tensor_reduce(gv[:, 5:6], gy[:, 1, :], AX_X, ALU.add))
                    link(nc.vector.tensor_scalar(gv[:, 6:7], gv[:, 5:6], -1.0 / D, None, ALU.mult))
                    link(nc.vector.tensor_scalar(gy[:, 2, :], gy[:, 1, :], gv[:, 6:7], None, ALU.add))
                    link(nc.vector.tensor_tensor(gy[:, 0, :], gy[:, 2, :], gy[:, 2, :], ALU.mult))
                    link(nc.vector.tensor_reduce(gv[:, 5:6], gy[:, 0, :], AX_X, ALU.add))
                    nc.vector.tensor_scalar(gv[:, 7:8], gv[:, 5:6], 1.0 / D, EPS, ALU.mult,
                                            ALU.add).then_inc(gen_var, 1)
                    dve.wait_ge(gen_dev, k + 1)
                    link(nc.vector.reciprocal(gv[:, 9:10], gv[:, 8:9]))
                    nc.vector.tensor_scalar(gy[:, 3, :], gy[:, 2, :], gv[:, 9:10], None, ALU.mult).then_inc(gen_res, 1)
                    assert chain[0] == STEPS

        @block.gpsimd
        def _(pool):
            nc.gpsimd.memset(ident[:, :], 0.0).then_inc(ones_ready, 1)
            nc.gpsimd.memset(xj[:, :, D:W], 1.0).then_inc(consts_ready, 1)
            pool.wait_ge(ones_ready, 1)
            nc.gpsimd.affine_select(out=ident[:, :], in_=ident[:, :], compare_op=ALU.not_equal, fill=1.0, base=0,
                                    pattern=[[-1, P]], channel_multiplier=1).then_inc(consts_ready, 1)
            nc.gpsimd.memset(ones[:, :], 1.0).then_inc(consts_ready, 1)
            nc.gpsimd.memset(eps[:, :], EPS).then_inc(consts_ready, 1)
            nc.gpsimd.memset(inv_d[:, :], 1.0 / D).then_inc(consts_ready, 1)
            for q in range(4):
                pool.wait_ge(xj_loaded[q], 16)
            pool.wait_ge(consts_ready, 5)
            half = NB // 2
            nc.gpsimd.tensor_tensor(tree[:, :, :], xj[:, 0:half, :], xj[:, half:NB, :], ALU.add).then_inc(tree_step, 1)
            pool.wait_ge(stats_ready, 1)
            nc.gpsimd.partition_all_reduce(top[:, :], stats[:, :], P, RMAX).then_inc(top_ready, 1)
            steps = 1
            while half > 1:
                half //= 2
                pool.wait_ge(tree_step, steps)
                ins = nc.gpsimd.tensor_tensor(tree[:, 0:half, :], tree[:, 0:half, :], tree[:, half:2 * half, :],
                                              ALU.add)
                ins.then_inc(tree_step if half > 1 else tree_ready, 1)
                steps += 1
            pool.wait_ge(xi_loaded, 16)
            pool.wait_ge(a_loaded, 32)
            nc.gpsimd.tensor_tensor(prod_i[:, :, :], xi[:, :, :].rearrange("p c (t d) -> p (c t) d", t=T),
                                    a_rows[:, 0:1, :].to_broadcast([P, NB, D]), ALU.mult).then_inc(prod_i_ready, 1)
            pool.wait_ge(ff_ready, 2)
            pool.wait_ge(sums_copied, 1)
            pool.sem_inc(sums_scaled, 1)
            STEPS = 7
            with pool.Fori(0, C) as c:
                chain = [0]

                def link(ins):
                    chain[0] += 1
                    ins.then_inc(pool_step, 1)
                    pool.wait_ge(pool_step, c * STEPS + chain[0])

                pool.wait_ge(sums_copied, c + 2)
                nc.gpsimd.tensor_tensor(scaled[:, :, :, :, :].rearrange("p t a h w -> p t a (h w)"),
                                        sums[:, :, :, :, :].rearrange("p t a h w -> p t a (h w)"),
                                        ff[:, bass.ds(c * T, T), :].unsqueeze(3).to_broadcast([P, T, 2, 2 * W]),
                                        ALU.mult).then_inc(sums_scaled, 1)
                pool.wait_ge(sums_scaled, c + 2)
                link(nc.gpsimd.tensor_tensor(planes[:, :, :, :].rearrange("p t h w -> p t (h w)"),
                                             scaled[:, :, 0, :, :].rearrange("p t h w -> p t (h w)"),
                                             scaled[:, :, 1, :, :].rearrange("p t h w -> p t (h w)"), ALU.add))
                nc.gpsimd.tensor_tensor(total[:, :, :], planes[:, :, 0, :], planes[:, :, 1, :],
                                        ALU.add).then_inc(total_ready, 1)
                pool.wait_ge(rden_ready, c + 1)
                link(nc.gpsimd.tensor_tensor(fill[:, :, :], mean_row[:, 0:D].unsqueeze(1).to_broadcast([P, T, D]),
                                             empty[:, :].unsqueeze(2).to_broadcast([P, T, D]), ALU.mult))
                link(nc.gpsimd.tensor_tensor(full[:, :, :], total[:, :, 0:D], fill[:, :, :], ALU.add))
                link(nc.gpsimd.tensor_tensor(att[:, :, :], full[:, :, :],
                                             rden[:, :].unsqueeze(2).to_broadcast([P, T, D]), ALU.mult))
                nc.gpsimd.tensor_tensor(z[:, :, :], att[:, :, :],
                                        xi[:, bass.ds(c, 1), :].rearrange("p c (t d) -> p (c t) d", t=T),
                                        ALU.add).then_inc(z_ready, 1)
                pool.wait_ge(zsum_ready, c + 1)
                link(nc.gpsimd.tensor_tensor(mean[:, :], zsum[:, :], inv_d[:, :], ALU.mult))
                link(nc.gpsimd.tensor_tensor(zc[:, :, :], z[:, :, :],
                                             mean[:, :].unsqueeze(2).to_broadcast([P, T, D]), ALU.subtract))
                nc.gpsimd.tensor_tensor(sq[:, :, :], zc[:, :, :], zc[:, :, :], ALU.mult).then_inc(sq_ready, 1)
                pool.wait_ge(rstd_ready, c + 1)
                link(nc.gpsimd.tensor_tensor(res[:, :, :], zc[:, :, :],
                                             rstd[:, :].unsqueeze(2).to_broadcast([P, T, D]), ALU.mult))
                pool.dma_start(out_i[c], res[:, :, :].rearrange("p t d -> p (t d)")).then_inc(res_stored, 16)
                pool.wait_ge(res_stored, (c + 1) * 16)
                assert chain[0] == STEPS


def kernel(x, adj, L0_gnn_a):
    import numpy as _np
    import concourse.bacc as _bacc
    from concourse import mybir as _mybir
    from concourse.bass_utils import run_bass_kernel_spmd as _run

    nc = _bacc.Bacc("TRN2", target_bir_lowering=False, num_devices=1)
    arrays, args = {}, []
    for name, value in (("x", x), ("adj", adj), ("a", L0_gnn_a)):
        value = _np.ascontiguousarray(value)
        arrays[f"in_{name}"] = value
        args.append(nc.dram_tensor(f"in_{name}", value.shape, _mybir.dt.from_np(value.dtype),
                                   kind="ExternalInput").ap())
    out = nc.dram_tensor("out_0", tuple(x.shape), _mybir.dt.float32, kind="ExternalOutput").ap()
    gat_layernorm(nc, *args, out)
    result = _run(nc, [arrays], core_ids=[0])
    return result.results[0]["out_0"]
```

```python
from contextlib import ExitStack

import concourse.bass as bass
from concourse import mybir
import numpy as np

ALU = mybir.AluOpType
ACT = mybir.ActivationFunctionType
AX_X = mybir.AxisListType.X
F32 = mybir.dt.float32
F16 = mybir.dt.float16
BF16 = mybir.dt.bfloat16
FP8 = mybir.dt.float8e4
I32 = mybir.dt.int32
RMAX = bass.bass_isa.ReduceOp.max

P = 128
SLOPE = 0.01
NEG_INF = -9000000000000000.0
EPS = 1e-5

ABOVE = 1.0
ABOVE_BYTE = 1.875
BELOW = float(np.array([0x00B80000], np.uint32).view(np.float32)[0])
BELOW_BYTE = -1.0

G_SCALE = 2048.0
MAX_SPREAD = 9.0
MIN_X, MAX_X = 0.5, 16.0
MAX_TOP = 60.0


def gat_layernorm(nc, x, adj, a, out):
    N, D = x.shape
    NB = N // P
    T = 4
    C = NB // T
    H = 2
    UW = N // H
    UB = UW // P
    U = T * H
    W = D + 1
    BANK = 512
    Q = 4
    HALF = NB // 2

    G = NB // 2
    x_b = x.rearrange("(g p q) d -> p g q d", p=P, q=2)
    out_b = out.rearrange("(g p q) d -> p g q d", p=P, q=2)
    adj_b = adj.rearrange("(g p q) j -> g q p j", p=P, q=2)
    a_row = a.rearrange("(a n) o -> o a n", a=2)
    a_col = a.rearrange("(a n) o -> n (a o)", a=2)

    with ExitStack() as ctx:
        def sb(name, shape, dt):
            return ctx.enter_context(nc.sbuf_tensor(name, shape, dt))

        def pb(name, shape, dt):
            return ctx.enter_context(nc.psum_tensor(name, shape, dt))

        def sem(name):
            return ctx.enter_context(nc.semaphore(name))

        CLEANS, CODES, TURNED = 4, 2, 2
        THRS = 2
        ring = sb("ring", [P, U, UW], I32)
        clean = sb("clean", [P, CLEANS, UW], BF16)
        thr = sb("thr", [P, THRS, N], BF16)
        code = sb("code", [P, CODES, UW], BF16)
        turned = sb("turned", [P, TURNED, UW], BF16)
        ident = sb("ident", [P, P], F32)
        ident16 = sb("ident16", [P, P], BF16)
        ident16h = sb("ident16h", [P, P], F16)
        ones = sb("ones", [P, P], F32)
        eps = sb("eps", [P, T], F32)
        inv_d = sb("inv_d", [P, T], F32)
        neg_half = sb("neg_half", [P, T], F32)
        xs = sb("xs", [P, NB, D], F32)
        d_all = sb("d_all", [P, N], F32)
        g = sb("g", [P, 2, NB, 2, W], F16)
        ns = sb("ns", [P, NB], F32)
        ratio = sb("ratio", [P, NB, 2], F32)
        mean_row = sb("mean_row", [P, D], F32)
        flag = sb("flag", [P, 1], I32)
        x16 = sb("x16", [P, NB, 2, D], F16)
        xt16 = sb("xt16", [P, N], F16)
        g32 = sb("g32", [P, 2, NB, W], F32)
        tree = sb("tree", [P, NB // 2, D], F32)
        a_rows = sb("a_rows", [P, 2, D], F32)
        a_cols = sb("a_cols", [P, 2], F32)
        a16 = sb("a16", [P, 2, 2], F16)
        a_rep = sb("a_rep", [P, 2, P], F16)
        sd = sb("sd", [P, 2, NB], F32)
        stats = sb("stats", [P, 4], F32)
        top = sb("top", [P, 4], F32)
        bias = sb("bias", [P, 2], F32)
        spread = sb("spread", [P, 6], F32)
        e12 = sb("e12", [P, 2, NB], F32)
        u = sb("u", [P, NB], F32)
        f = sb("f", [P, NB], F32)
        both = sb("both", [P, T, 2, 2 * W], F32)
        total = sb("total", [P, T, W], F32)
        empty = sb("empty", [P, T], F32)
        den = sb("den", [P, T], F32)
        rden = sb("rden", [P, T], F32)
        fill = sb("fill", [P, T, D], F32)
        full = sb("full", [P, T, D], F32)
        att = sb("att", [P, T, D], F32)
        z = sb("z", [P, T, D], F32)
        zsum = sb("zsum", [P, T], F32)
        mean = sb("mean", [P, T], F32)
        zc = sb("zc", [P, T, D], F32)
        sq = sb("sq", [P, T, D], F32)
        vsum = sb("vsum", [P, T], F32)
        vmean = sb("vmean", [P, T], F32)
        var = sb("var", [P, T], F32)
        rstd = sb("rstd", [P, T], F32)
        res = sb("res", [P, T, D], F32)
        spare = x16.rearrange("p b h d -> p (b h d)").bitcast(F32)
        last_total = spare[:, 0:T * W].rearrange("p (t w) -> p t w", t=T)
        last_full, last_z, last_res = (spare[:, T * (W + k * D):T * (W + (k + 1) * D)].rearrange("p (t d) -> p t d", t=T)
                                       for k in range(3))
        last_empty = sb("last_empty", [P, T], F32)
        last_den = sb("last_den", [P, T], F32)
        last_rden = sb("last_rden", [P, T], F32)
        last_stats = sb("last_stats", [P, T, 6], F32)
        last_mean_var = sb("last_mean_var", [P, T, 2], F32)
        last_var = sb("last_var", [P, T], F32)
        last_rstd = sb("last_rstd", [P, T], F32)
        gadj, ge, gt = (ring[:, k * H:(k + 1) * H, :].rearrange("p h w -> p (h w)") for k in range(3))
        ge, gt = ge.bitcast(F32), gt.bitcast(F32)
        gv = sb("gv", [P, 10], F32)
        gxt = gt[0:D, 0:BANK]
        gen_rep = gt[0:D, BANK:BANK + P]
        gx = att[:, 0, :]
        gy = sq

        pt = pb("pt", [P, 2, 2 * UW // 2], BF16)
        acc = pb("acc", [P, T, BANK], F32)

        def words(ap):
            return ap.bitcast(F32)

        def rows_of(ap, b):
            return ap[:, (b // 2) * 2 * P:(b // 2 + 1) * 2 * P].rearrange("p (i q) -> p q i", q=2)[:, b % 2, :]

        def early_bank(k):
            return acc[:, k, :] if k < T else pt[:, (k - T) // 2, :].bitcast(F32)[:, (k % 2) * BANK:(k % 2 + 1) * BANK]

        x_loaded = [sem(f"x_loaded{q}") for q in range(Q)]
        a_loaded = sem("a_loaded")
        zeroed = sem("zeroed")
        x_high = sem("x_high")
        x_low = [sem(f"x_low{q}") for q in range(Q)]
        a16_step = sem("a16_step")
        a_rep_ready = sem("a_rep_ready")
        x_transposed = sem("x_transposed")
        xt_copied = sem("xt_copied")
        sd_summed = sem("sd_summed")
        sd_ready = sem("sd_ready")
        ns_ready = sem("ns_ready")
        consts_ready = sem("consts_ready")
        d_summed = sem("d_summed")
        d_copied = sem("d_copied")
        stats_ready = sem("stats_ready")
        top_ready = sem("top_ready")
        bias_ready = sem("bias_ready")
        e_ready = sem("e_ready")
        e_scaled = sem("e_scaled")
        g32_ready = [sem(f"g32_ready{half}") for half in range(2)]
        g32_by_pool = sem("g32_by_pool")
        ghi_ready = [sem(f"ghi_ready{half}") for half in range(2)]
        glo_ready = [sem(f"glo_ready{half}") for half in range(2)]
        flag_step = sem("flag_step")
        flag_ready = sem("flag_ready")
        u_ready = sem("u_ready")
        f_ready = sem("f_ready")
        ratio_ready = sem("ratio_ready")
        tree_step = sem("tree_step")
        tree_ready = sem("tree_ready")
        mean_summed = sem("mean_summed")
        mean_ready = sem("mean_ready")
        unit_loaded = [sem(f"unit_loaded{m}") for m in range(U)]
        clean_ready = sem("clean_ready")
        thr_ready = sem("thr_ready")
        code_ready = sem("code_ready")
        transposed = sem("transposed")
        turned_ready = sem("turned_ready")
        products_done = sem("products_done")
        sums_taken = sem("sums_taken")
        total_ready = sem("total_ready")
        den_step = sem("den_step")
        rden_ready = sem("rden_ready")
        rows_step = sem("rows_step")
        z_ready = sem("z_ready")
        zsum_ready = sem("zsum_ready")
        sq_ready = sem("sq_ready")
        vsum_ready = sem("vsum_ready")
        rstd_ready = sem("rstd_ready")
        res_ready = sem("res_ready")
        res_stored = sem("res_stored")
        last_step = sem("last_step")
        last_var_ready = sem("last_var_ready")
        last_rstd_ready = sem("last_rstd_ready")
        last_res_ready = sem("last_res_ready")
        last_stored = sem("last_stored")
        gen_ready = sem("gen_ready")
        gen_xt = sem("gen_xt")
        gen_d = sem("gen_d")
        gen_loaded = sem("gen_loaded")
        gen_step = sem("gen_step")
        gen_masked = sem("gen_masked")
        gen_weights = sem("gen_weights")
        gen_turned = sem("gen_turned")
        gen_copied = sem("gen_copied")
        gen_summed = sem("gen_summed")
        gen_var = sem("gen_var")
        gen_dev = sem("gen_dev")
        gen_res = sem("gen_res")
        gen_stored = sem("gen_stored")

        block = ctx.enter_context(nc.Block())

        def general(eng):
            eng.wait_ge(flag_ready, 1)
            return eng.If(eng.value_load(flag[0:1, 0:1], min_val=0, max_val=1) > 0)

        def unit(c, m):
            return (c, m) if m < U else (c + 1, m - U)

        def at(c, m, back=0):
            n = c * U + (m + 1 - back)
            return None if isinstance(n, int) and n < 1 else n

        def pairs(ap):
            return ap.rearrange("p (g q) d -> p g q d", q=2)

        def tile_rows(c, t):
            return adj_b[c * (T // 2) + t // 2, t % 2]

        def tile(c, t):
            n = c * T + t
            return slice(n, n + 1) if isinstance(n, int) else bass.ds(n, 1)

        @block.sync
        def _(sp):
            bq = NB // Q
            for q in range(Q):
                sp.dma_start(pairs(xs)[:, q * bq // 2:(q + 1) * bq // 2], x_b[:, q * bq // 2:(q + 1) * bq // 2])\
                    .then_inc(x_loaded[q], 16)

            def load(c, m):
                sp.dma_start(ring[:, m, :], tile_rows(c, m // H)[:, (m % H) * UW:(m % H + 1) * UW])\
                    .then_inc(unit_loaded[m], 16)

            for m in range(U):
                load(0, m)
            with sp.Fori(1, C) as c:
                for m in range(U):
                    sp.wait_ge(clean_ready, c * U + (m + 1 - U))
                    load(c, m)
            for t in range(T):
                sp.wait_ge(last_res_ready, t + 1)
                sp.dma_start(out_b[:, (C - 1) * (T // 2) + t // 2, t % 2, :], last_res[:, t, :])\
                    .then_inc(last_stored, 16)
            sp.wait_ge(last_stored, T * 16)
            with general(sp):

                def load_tile(k):
                    sp.dma_start(gadj, adj.rearrange("(k p) j -> k p j", p=P)[k]).then_inc(gen_loaded, 16)
                    sp.dma_start(gx, x.rearrange("(k p) d -> k p d", p=P)[k]).then_inc(gen_loaded, 16)

                def store_tile(k):
                    sp.wait_ge(gen_res, k + 1)
                    sp.dma_start(out.rearrange("(k p) d -> k p d", p=P)[k], gy[:, 3, :]).then_inc(gen_stored, 16)
                    sp.wait_ge(gen_stored, (k + 1) * 16)

                load_tile(0)
                with sp.Fori(0, NB - 1) as k:
                    store_tile(k)
                    load_tile(k + 1)
                store_tile(NB - 1)

        @block.tensor
        def _(pe):
            def products_wait(c, m):
                pe.wait_ge(turned_ready, at(c, m))
                if m % H == 0:
                    pe.wait_ge(sums_taken, c * T + (m // H + 1))

            def transposes(c, m, then=None):
                c, m = unit(c, m)
                pe.wait_ge(code_ready, at(c, m))
                if at(c, m, 2) is not None:
                    pe.wait_ge(turned_ready, at(c, m, 2))
                for b in range(UB):
                    if then and b == UB - 1:
                        products_wait(*unit(*then))
                    last = nc.tensor.transpose(pt[:, m % 2, b * P:(b + 1) * P],
                                               rows_of(code[:, m % CODES, :], b), ident16[:, :])
                last.then_inc(transposed, 1)

            def products(c, m):
                t = m // H
                for b in range(UB):
                    blk = (m % H) * UB + b
                    planes = turned[:, m % TURNED, b * P:(b + 1) * P].bitcast(FP8).rearrange("p (i h) -> p h i", h=2)
                    nc.tensor.matmul(acc[:, t, 0:2 * W], planes[:, 1, :],
                                     g[:, 0, blk, :, :].rearrange("p h w -> p (h w)"),
                                     start=(blk == 0), stop=(blk == NB - 1), skip_group_check=True)
                    last = nc.tensor.matmul(acc[:, t, 2 * W:4 * W], planes[:, 0, :],
                                            g[:, 1, blk, :, :].rearrange("p h w -> p (h w)"),
                                            start=False, stop=(blk == NB - 1), skip_group_check=True)
                last.then_inc(products_done, 1)

            pe.wait_ge(consts_ready, 8)
            for q in range(Q):
                pe.wait_ge(x_high, q + 1)
                pe.wait_ge(x_low[q], 1)
                for b in range(NB // Q):
                    last = nc.tensor.transpose(early_bank(q).bitcast(F16)[:, b * P:(b + 1) * P],
                                               x16[:, q * (NB // Q) + b, :, :].rearrange("p h d -> p (h d)"),
                                               ident16h[:, :])
                last.then_inc(x_transposed, 1)
            pe.wait_ge(a_rep_ready, 2)
            for q in range(Q):
                pe.wait_ge(xt_copied, q + 1)
                for b in range(q * NB // Q, (q + 1) * NB // Q):
                    last = nc.tensor.matmul(early_bank(7)[:, 4 * b:4 * b + 4], xt16[:, b * P:(b + 1) * P],
                                            a16[:, :, :].rearrange("p h a -> p (h a)"), start=True, stop=True)
            last.then_inc(sd_summed, 1)
            in_order = xt16.rearrange("p (g q i) -> p g i q", q=2, i=P)
            for k in range(N // BANK):
                if k >= 3:
                    pe.wait_ge(d_copied, k - 2)
                for h in range(2):
                    last = nc.tensor.matmul(early_bank(T + k % 3), a_rep[:, h, :], in_order[:, 2 * k:2 * k + 2],
                                            start=(h == 0), stop=(h == 1))
                last.then_inc(d_summed, 1)
            pe.wait_ge(tree_ready, 1)
            nc.tensor.matmul(early_bank(T - 1)[:, 0:D], ones[:, :], tree[:, 0, :], start=True, stop=True)\
                .then_inc(mean_summed, 1)
            pe.wait_ge(d_copied, N // BANK)
            pe.wait_ge(sd_ready, 1)
            pe.wait_ge(mean_ready, 1)
            transposes(0, 0)
            transposes(0, 1)
            for m in range(H):
                pe.wait_ge(glo_ready[m], 2)
                products_wait(0, m)
                products(0, m)
            transposes(0, 2)
            transposes(0, 3, (0, 2))
            for m in range(2, U):
                products(0, m)
                transposes(0, m + 2, (0, m + 1))

            with pe.Fori(1, C - 1) as c:
                for m in range(U):
                    products(c, m)
                    transposes(c, m + 2, (c, m + 1))
            for m in range(U):
                products(C - 1, m)
                if m + 2 < U:
                    transposes(C - 1, m + 2, (C - 1, m + 1))
                elif m + 1 < U:
                    products_wait(C - 1, m + 1)

            with general(pe):
                pe.wait_ge(gen_ready, 1)
                for k in range(N // BANK):
                    if k >= 1:
                        pe.wait_ge(gen_d, 2 * k)
                    for b in range(4):
                        last = nc.tensor.transpose(rows_of(early_bank(T)[0:D, :], b), xs[:, 4 * k + b, :],
                                                   ident[:, :])
                    last.then_inc(gen_xt, 1)
                    pe.wait_ge(gen_d, 2 * k + 1)
                    nc.tensor.matmul(early_bank(T + 2), gen_rep[:, :], gxt[:, :], start=True, stop=True)\
                        .then_inc(gen_xt, 1)
                pe.wait_ge(gen_d, 2 * (N // BANK))
                with pe.Fori(0, NB) as k:
                    pe.wait_ge(gen_weights, k + 1)
                    for h in range(4):
                        if h >= 1:
                            pe.wait_ge(gen_copied, k * 4 + h)
                        for b in range(8):
                            last = nc.tensor.transpose(early_bank(T + b // 4)[:, (b % 4) * P:(b % 4 + 1) * P],
                                                       rows_of(ge, h * 8 + b), ident[:, :])
                        last.then_inc(gen_turned, 1)
                    pe.wait_ge(gen_copied, k * 4 + 4)
                    for b in range(NB):
                        last = nc.tensor.matmul(acc[:, 0, 0:D], gt[:, b * P:(b + 1) * P], xs[:, b, :],
                                                start=(b == 0), stop=(b == NB - 1))
                    last.then_inc(gen_summed, 1)

        @block.scalar
        def _(act):
            with nc.allow_non_contiguous_dma(reason="256 bytes of a"):
                act.dma_start(a_cols[0:D, :], a_col).then_inc(a_loaded, 16)
            with nc.allow_non_contiguous_dma(reason="256 bytes of a"):
                act.dma_start(a_cols[D:P, :], a_col).then_inc(a_loaded, 16)
            act.dma_start(a_rows[:, :, :], a_row.to_broadcast([P, 2, D])).then_inc(a_loaded, 16)

            def clean_adj(c, m):
                c, m = unit(c, m)
                act.wait_ge(unit_loaded[m], (c + 1) * 16)
                if at(c, m, CLEANS) is not None:
                    act.wait_ge(code_ready, at(c, m, CLEANS))
                nc.scalar.activation(clean[:, m % CLEANS, :], ring[:, m, :], ACT.Relu).then_inc(clean_ready, 1)

            AHEAD = 3

            def turn(c, m):
                act.wait_ge(transposed, at(c, m))
                if at(c, m, TURNED) is not None:
                    act.wait_ge(products_done, at(c, m, TURNED))
                nc.scalar.copy(words(turned[:, m % TURNED, :]), words(pt[:, m % 2, :])).then_inc(turned_ready, 1)

            for q in range(Q):
                act.wait_ge(x_transposed, q + 1)
                nc.scalar.copy(words(xt16[:, q * (N // Q):(q + 1) * (N // Q)]), early_bank(q)).then_inc(xt_copied, 1)

            def copy_d(k):
                act.wait_ge(d_summed, k + 1)
                nc.scalar.copy(d_all[:, k * BANK:(k + 1) * BANK], early_bank(T + k % 3)).then_inc(d_copied, 1)

            for k in range(2):
                copy_d(k)
            act.wait_ge(bias_ready, 2)
            nc.scalar.activation(e12[:, 0, :], sd[:, 1, :], ACT.Exp, bias=bias[:, 0:1], scale=1.0)\
                .then_inc(e_ready, 1)
            nc.scalar.activation(e12[:, 1, :], sd[:, 1, :], ACT.Exp, bias=bias[:, 1:2], scale=SLOPE)\
                .then_inc(e_ready, 1)
            for k in range(2, N // BANK):
                copy_d(k)
            act.wait_ge(u_ready, 1)
            nc.scalar.activation(f[:, :], u[:, :], ACT.Exp, scale=1.0 - SLOPE).then_inc(f_ready, 1)
            act.wait_ge(f_ready, 1)
            nc.scalar.mul(ratio[:, :, 0], f[:, :], BELOW_BYTE / ABOVE_BYTE).then_inc(ratio_ready, 1)
            act.wait_ge(mean_summed, 1)
            nc.scalar.copy(mean_row[:, :], early_bank(T - 1)[:, 0:D]).then_inc(mean_ready, 1)
            for m in range(AHEAD):
                clean_adj(0, m)

            def chunk(c, last=False):
                for m in range(U):
                    turn(c, m)
                    if not (last and m + AHEAD >= U):
                        clean_adj(c, m + AHEAD)

            chunk(0)
            with act.Fori(1, C - 1) as c:
                chunk(c)
            chunk(C - 1, last=True)

            with general(act):
                with act.Fori(0, NB) as k:
                    act.wait_ge(gen_masked, k + 1)
                    nc.scalar.activation(ge, ge, ACT.Exp, bias=gv[:, 2:3], scale=1.0,
                                         accum_out=gv[:, 3:4]).then_inc(gen_weights, 1)
                    act.wait_ge(gen_var, k + 1)
                    nc.scalar.activation(gv[:, 8:9], gv[:, 7:8], ACT.Sqrt).then_inc(gen_dev, 1)

        def rows_out(eng, ops, c, link):
            eng.wait_ge(rden_ready, c + 1)
            link(ops.tensor_tensor(fill[:, :, :], mean_row[:, :].unsqueeze(1).to_broadcast([P, T, D]),
                                   empty[:, :].unsqueeze(2).to_broadcast([P, T, D]), ALU.mult))
            link(ops.tensor_tensor(full[:, :, :], total[:, :, 0:D], fill[:, :, :], ALU.add))
            link(ops.tensor_tensor(att[:, :, :], full[:, :, :], rden[:, :].unsqueeze(2).to_broadcast([P, T, D]),
                                   ALU.mult))
            rows = slice(c * T, (c + 1) * T) if isinstance(c, int) else bass.ds(c * T, T)
            ops.tensor_tensor(z[:, :, :], att[:, :, :], xs[:, rows, 0:D], ALU.add).then_inc(z_ready, 1)

        def centre(eng, ops, c, link):
            eng.wait_ge(zsum_ready, c + 1)
            link(ops.tensor_tensor(mean[:, :], zsum[:, :], inv_d[:, :], ALU.mult))
            link(ops.tensor_tensor(zc[:, :, :], z[:, :, :], mean[:, :].unsqueeze(2).to_broadcast([P, T, D]),
                                   ALU.subtract))
            ops.tensor_tensor(sq[:, :, :], zc[:, :, :], zc[:, :, :], ALU.mult).then_inc(sq_ready, 1)

        ROWS_STEPS = 9

        @block.vector
        def _(dve):
            def threshold(c, t):
                c, t = (c, t) if t < T else (c + 1, t - T)
                if at(c, t * H + H - 1, THRS * H) is not None:
                    dve.wait_ge(code_ready, at(c, t * H + H - 1, THRS * H))
                nc.vector.tensor_scalar(thr[:, t % THRS, :], d_all[:, :], ns[:, tile(c, t)], BELOW,
                                        ALU.is_gt, ALU.max).then_inc(thr_ready, 1)

            def combine(c, m):
                t, half = m // H, slice((m % H) * UW, (m % H + 1) * UW)
                dve.wait_ge(thr_ready, c * T + (t + 1))
                dve.wait_ge(clean_ready, at(c, m))
                if at(c, m, CODES) is not None:
                    dve.wait_ge(transposed, at(c, m, CODES))
                nc.vector.tensor_tensor(code[:, m % CODES, :], clean[:, m % CLEANS, :], thr[:, t % THRS, half],
                                        ALU.min).then_inc(code_ready, 1)

            def take_sums(c, t):
                dve.wait_ge(products_done, at(c, t * H + H - 1))
                if t == 0 and not (isinstance(c, int) and c == 0):
                    dve.wait_ge(total_ready, c)
                nc.vector.tensor_tensor(both[:, t, :, :],
                                        acc[:, t, 0:4 * W].rearrange("p (w k) -> p w k", w=2),
                                        ratio[:, tile(c, t), :].rearrange("p o w -> p (o w)").unsqueeze(2)
                                        .to_broadcast([P, 2, 2 * W]), ALU.mult).then_inc(sums_taken, 1)

            def recip_den(c):
                dve.wait_ge(total_ready, c + 1)
                nc.vector.tensor_scalar(empty[:, :], total[:, :, D], 0.0, None, ALU.is_equal).then_inc(den_step, 1)
                dve.wait_ge(den_step, c * 2 + 1)
                nc.vector.scalar_tensor_tensor(out=den[:, :], in0=empty[:, :], scalar=float(N), in1=total[:, :, D],
                                               op0=ALU.mult, op1=ALU.add).then_inc(den_step, 1)
                dve.wait_ge(den_step, c * 2 + 2)
                nc.vector.reciprocal(rden[:, :], den[:, :]).then_inc(rden_ready, 1)

            def sum_z(c):
                dve.wait_ge(z_ready, c + 1)
                nc.vector.tensor_reduce(zsum[:, :], z[:, :, :], AX_X, ALU.add).then_inc(zsum_ready, 1)

            def sum_sq(c):
                dve.wait_ge(sq_ready, c + 1)
                nc.vector.tensor_reduce(vsum[:, :], sq[:, :, :], AX_X, ALU.add).then_inc(vsum_ready, 1)

            dve.sem_inc(sums_taken, T)
            for q in range(Q):
                dve.wait_ge(x_loaded[q], 16)
                bs = slice(q * (NB // Q), (q + 1) * (NB // Q))
                nc.vector.tensor_copy(x16[:, bs, 0, :], xs[:, bs, :]).then_inc(x_high, 1)
                if q == 1:
                    dve.wait_ge(a_loaded, 48)
                    nc.vector.tensor_copy(a16[:, 0, :], a_cols[:, :]).then_inc(a16_step, 1)
                    dve.wait_ge(a16_step, 1)
                    nc.vector.tensor_tensor(a16[:, 1, :], a_cols[:, :], a16[:, 0, :], ALU.subtract).then_inc(a16_step, 1)
                    dve.wait_ge(a16_step, 2)
                    for h in range(2):
                        nc.vector.tensor_copy(a_rep[:, h, :], a16[:, h, 1:2].to_broadcast([P, P])).then_inc(a_rep_ready, 1)
                if q % 2 == 1:
                    dve.wait_ge(x_high, q + 1)
                    nc.vector.tensor_tensor(x16[:, bs, 1, :], xs[:, bs, :], x16[:, bs, 0, :],
                                            ALU.subtract).then_inc(x_low[q], 1)
            nc.vector.tensor_reduce(stats[:, 2:3], xs[:, :, :], mybir.AxisListType.XY, ALU.max,
                                    apply_absolute_value=True)
            dve.wait_ge(sd_summed, 1)
            nc.vector.tensor_reduce(sd[:, :, :], early_bank(7)[:, 0:4 * NB].rearrange("p (b h a) -> p a b h", h=2, a=2),
                                    AX_X, ALU.add).then_inc(sd_ready, 1)
            dve.wait_ge(sd_ready, 1)
            nc.vector.tensor_reduce(stats[:, 0:1], sd[:, 1, :], AX_X, ALU.max)
            nc.vector.tensor_reduce(stats[:, 3:4], sd[:, 0, :], AX_X, ALU.max)
            nc.vector.tensor_reduce(stats[:, 1:2], sd[:, 1, :], AX_X, ALU.min, negate=True).then_inc(stats_ready, 1)
            nc.vector.tensor_scalar(ns[:, :], sd[:, 0, :], -1.0, None, ALU.mult).then_inc(ns_ready, 1)
            dve.wait_ge(top_ready, 1)
            nc.vector.tensor_scalar(bias[:, 0:1], top[:, 0:1], -1.0, None, ALU.mult).then_inc(bias_ready, 1)
            nc.vector.tensor_scalar(bias[:, 1:2], top[:, 0:1], -SLOPE, None, ALU.mult).then_inc(bias_ready, 1)
            nc.vector.tensor_scalar(u[:, :], sd[:, 0, :], top[:, 0:1], None, ALU.add).then_inc(u_ready, 1)
            dve.wait_ge(e_ready, 2)
            nc.vector.tensor_scalar(e12[:, :, :], e12[:, :, :], G_SCALE, None, ALU.mult).then_inc(e_scaled, 1)
            dve.wait_ge(e_scaled, 1)
            nc.vector.tensor_copy(g32[:, :, :, D], e12[:, :, :]).then_inc(e_scaled, 1)

            def scale_x(w, half):
                bs = slice(half * HALF, (half + 1) * HALF)
                nc.vector.tensor_tensor(g32[:, w, bs, 0:D], xs[:, bs, :],
                                        e12[:, w, bs].unsqueeze(2).to_broadcast([P, HALF, D]),
                                        ALU.mult).then_inc(g32_ready[half], 1)

            def high_part(w, half):
                bs = slice(half * HALF, (half + 1) * HALF)
                if (w, half) == (1, 1):
                    dve.wait_ge(g32_by_pool, 1)
                else:
                    dve.wait_ge(g32_ready[half], w + 1)
                nc.vector.tensor_copy(g[:, w, bs, 0, :], g32[:, w, bs, :]).then_inc(ghi_ready[half], 1)

            for w in range(2):
                scale_x(w, 0)
                dve.wait_ge(e_scaled, 2)
                high_part(w, 0)
            dve.wait_ge(d_copied, N // BANK)
            dve.wait_ge(ns_ready, 1)
            threshold(0, 0)
            combine(0, 0)
            combine(0, 1)
            scale_x(0, 1)
            high_part(0, 1)
            high_part(1, 1)
            dve.wait_ge(ghi_ready[1], 2)
            nc.vector.tensor_tensor(g[:, 1, HALF:NB, 1, :], g32[:, 1, HALF:NB, :], g[:, 1, HALF:NB, 0, :],
                                    ALU.subtract).then_inc(glo_ready[1], 1)
            dve.wait_ge(ratio_ready, 1)

            def raise_flag():
                nc.vector.tensor_scalar(spread[:, 0:1], top[:, 0:1], top[:, 1:2], MAX_SPREAD, ALU.add,
                                        ALU.is_le).then_inc(flag_step, 1)
                nc.vector.tensor_scalar(spread[:, 1:2], top[:, 2:3], MIN_X, None, ALU.is_ge).then_inc(flag_step, 1)
                nc.vector.tensor_scalar(spread[:, 2:3], top[:, 0:1], top[:, 3:4], MAX_TOP, ALU.add,
                                        ALU.is_le).then_inc(flag_step, 1)
                dve.wait_ge(flag_step, 3)
                nc.vector.scalar_tensor_tensor(out=spread[:, 3:4], in0=top[:, 2:3], scalar=MAX_X,
                                               in1=spread[:, 1:2], op0=ALU.is_le,
                                               op1=ALU.mult).then_inc(flag_step, 1)
                nc.vector.tensor_tensor(spread[:, 4:5], spread[:, 0:1], spread[:, 2:3],
                                        ALU.mult).then_inc(flag_step, 1)
                dve.wait_ge(flag_step, 5)
                nc.vector.tensor_tensor(spread[:, 5:6], spread[:, 3:4], spread[:, 4:5],
                                        ALU.mult).then_inc(flag_step, 1)
                dve.wait_ge(flag_step, 6)
                nc.vector.tensor_scalar(flag[:, :], spread[:, 5:6], -1.0, 1.0, ALU.mult,
                                        ALU.add).then_inc(flag_ready, 1)

            def chunk(c, first=False, last=False):
                for m in range(U):
                    if not (first and m < 2):
                        combine(c, m)
                    if m % H == 0 and not (last and m // H + 1 == T):
                        threshold(c, m // H + 1)
                    if m in (1, 3) and not first:
                        take_sums(c - 1, T - 2 + m // 2)
                    if not first:
                        if m == 4:
                            recip_den(c - 1)
                        if m == 6:
                            sum_z(c - 1)
                        if m == 7:
                            sum_sq(c - 1)
                    elif m == 3:
                        raise_flag()
                    if m in (5, 7):
                        take_sums(c, m // 2 - 2)
                    if last and m == 7:
                        last_rows(0)

            done = [0]

            def link(ins):
                done[0] += 1
                ins.then_inc(last_step, 1)
                dve.wait_ge(last_step, done[0])

            def last_rows(t):
                one = slice(t, t + 1)
                dve.wait_ge(sums_taken, T + (C - 1) * T + t + 1)
                link(nc.vector.tensor_tensor(both[:, t, 0, :], both[:, t, 0, :], both[:, t, 1, :], ALU.add))
                link(nc.vector.tensor_tensor(last_total[:, t, :], both[:, t, 0, 0:W], both[:, t, 0, W:2 * W],
                                             ALU.add))
                link(nc.vector.tensor_scalar(last_empty[:, one], last_total[:, t, D:W], 0.0, None, ALU.is_equal))
                link(nc.vector.scalar_tensor_tensor(out=last_den[:, one], in0=last_empty[:, one], scalar=float(N),
                                                    in1=last_total[:, t, D:W], op0=ALU.mult, op1=ALU.add))
                nc.vector.reciprocal(last_rden[:, one], last_den[:, one])
                link(nc.vector.scalar_tensor_tensor(out=last_full[:, t, :], in0=mean_row[:, :],
                                                    scalar=last_empty[:, one], in1=last_total[:, t, 0:D],
                                                    op0=ALU.mult, op1=ALU.add))
                link(nc.vector.scalar_tensor_tensor(out=last_z[:, t, :], in0=last_full[:, t, :],
                                                    scalar=last_rden[:, one], in1=xs[:, (C - 1) * T + t, :],
                                                    op0=ALU.mult, op1=ALU.add))
                link(nc.vector.bn_stats(last_stats[:, t, :], last_z[:, t, :]))
                link(nc.vector.bn_aggr(last_mean_var[:, t, :], last_stats[:, t, :]))
                nc.vector.tensor_scalar(last_var[:, one], last_mean_var[:, t, 1:2], EPS, None,
                                        ALU.add).then_inc(last_var_ready, 1)

            def last_scale(t):
                dve.wait_ge(last_rstd_ready, t + 1)
                nc.vector.tensor_scalar(last_res[:, t, :], last_z[:, t, :], last_mean_var[:, t, 0:1],
                                        last_rstd[:, t:t + 1], ALU.subtract, ALU.mult).then_inc(last_res_ready, 1)

            chunk(0, first=True)
            with dve.Fori(1, C - 1) as c:
                chunk(c)
            chunk(C - 1, last=True)
            last_rows(1)
            take_sums(C - 1, 2)
            last_scale(0)
            last_rows(2)
            last_scale(1)
            take_sums(C - 1, 3)
            last_scale(2)
            last_rows(3)
            last_scale(3)

            with general(dve):
                dve.wait_ge(clean_ready, C * U)
                nc.vector.tensor_copy(gen_rep, a_cols[0:D, 1:2].to_broadcast([D, P])).then_inc(gen_ready, 1)
                for k in range(N // BANK):
                    dve.wait_ge(gen_xt, 2 * k + 1)
                    nc.vector.tensor_copy(gxt, early_bank(T)[0:D, :]).then_inc(gen_d, 1)
                    dve.wait_ge(gen_xt, 2 * k + 2)
                    nc.vector.tensor_copy(d_all[:, k * BANK:(k + 1) * BANK], early_bank(T + 2)).then_inc(gen_d, 1)
                dve.wait_ge(gen_d, 2 * (N // BANK))
                STEPS = 16
                with dve.Fori(0, NB) as k:
                    chain = [0]

                    def glink(ins):
                        chain[0] += 1
                        ins.then_inc(gen_step, 1)
                        dve.wait_ge(gen_step, k * STEPS + chain[0])

                    dve.wait_ge(gen_loaded, (k + 1) * 32)
                    glink(nc.vector.tensor_tensor(gy[:, 0, :], gx, a_rows[:, 0, :], ALU.mult))
                    glink(nc.vector.tensor_reduce(gv[:, 0:1], gy[:, 0, :], AX_X, ALU.add))
                    glink(nc.vector.tensor_scalar(gt, d_all[:, :], gv[:, 0:1], None, ALU.add))
                    glink(nc.vector.scalar_tensor_tensor(out=ge, in0=gt, scalar=SLOPE, in1=gt,
                                                         op0=ALU.mult, op1=ALU.max))
                    glink(nc.vector.scalar_tensor_tensor(out=gt, in0=gadj, scalar=0.0, in1=ge,
                                                         op0=ALU.is_gt, op1=ALU.mult))
                    glink(nc.vector.tensor_scalar(ge, gadj, 0.0, -1.0, ALU.is_gt, ALU.add))
                    glink(nc.vector.scalar_tensor_tensor(out=ge, in0=ge, scalar=-NEG_INF, in1=gt,
                                                         op0=ALU.mult, op1=ALU.add))
                    glink(nc.vector.tensor_reduce(gv[:, 1:2], ge, AX_X, ALU.max))
                    nc.vector.tensor_scalar(gv[:, 2:3], gv[:, 1:2], -1.0, None, ALU.mult).then_inc(gen_masked, 1)
                    for h in range(4):
                        dve.wait_ge(gen_turned, k * 4 + h + 1)
                        nc.vector.tensor_copy(gt[:, h * 1024:(h + 1) * 1024],
                                              pt[:, 0, :].bitcast(F32)).then_inc(gen_copied, 1)
                    dve.wait_ge(gen_summed, k + 1)
                    glink(nc.vector.reciprocal(gv[:, 4:5], gv[:, 3:4]))
                    glink(nc.vector.scalar_tensor_tensor(out=gy[:, 1, :], in0=acc[:, 0, 0:D], scalar=gv[:, 4:5],
                                                         in1=gx, op0=ALU.mult, op1=ALU.add))
                    glink(nc.vector.tensor_reduce(gv[:, 5:6], gy[:, 1, :], AX_X, ALU.add))
                    glink(nc.vector.tensor_scalar(gv[:, 6:7], gv[:, 5:6], -1.0 / D, None, ALU.mult))
                    glink(nc.vector.tensor_scalar(gy[:, 2, :], gy[:, 1, :], gv[:, 6:7], None, ALU.add))
                    glink(nc.vector.tensor_tensor(gy[:, 0, :], gy[:, 2, :], gy[:, 2, :], ALU.mult))
                    glink(nc.vector.tensor_reduce(gv[:, 5:6], gy[:, 0, :], AX_X, ALU.add))
                    nc.vector.tensor_scalar(gv[:, 7:8], gv[:, 5:6], 1.0 / D, EPS, ALU.mult,
                                            ALU.add).then_inc(gen_var, 1)
                    dve.wait_ge(gen_dev, k + 1)
                    glink(nc.vector.reciprocal(gv[:, 9:10], gv[:, 8:9]))
                    nc.vector.tensor_scalar(gy[:, 3, :], gy[:, 2, :], gv[:, 9:10], None, ALU.mult).then_inc(gen_res, 1)
                    assert chain[0] == STEPS

        @block.gpsimd
        def _(pool):
            for square in (ident16h, ident16, ident):
                nc.gpsimd.memset(square[:, :], 0.0).then_inc(zeroed, 1)
            nc.gpsimd.memset(ones[:, :], 1.0).then_inc(consts_ready, 1)
            nc.gpsimd.memset(ratio[:, :, 1], 1.0).then_inc(consts_ready, 1)
            nc.gpsimd.memset(eps[:, :], EPS).then_inc(consts_ready, 1)
            nc.gpsimd.memset(inv_d[:, :], 1.0 / D).then_inc(consts_ready, 1)
            nc.gpsimd.memset(neg_half[:, :], -0.5).then_inc(consts_ready, 1)
            pool.wait_ge(zeroed, 3)
            for square in (ident16h, ident16, ident):
                nc.gpsimd.affine_select(out=square[:, :], in_=square[:, :], compare_op=ALU.not_equal, fill=1.0,
                                        base=0, pattern=[[-1, P]], channel_multiplier=1).then_inc(consts_ready, 1)
            for q in (0, 2):
                pool.wait_ge(x_high, q + 1)
                bs = slice(q * (NB // Q), (q + 1) * (NB // Q))
                nc.gpsimd.tensor_tensor(x16[:, bs, 1, :], xs[:, bs, :], x16[:, bs, 0, :],
                                        ALU.subtract).then_inc(x_low[q], 1)
            pool.wait_ge(x_high, Q)
            half = NB // 2
            nc.gpsimd.tensor_tensor(tree[:, :, :], xs[:, 0:half, :], xs[:, half:NB, :], ALU.add).then_inc(tree_step, 1)
            pool.wait_ge(stats_ready, 1)
            nc.gpsimd.partition_all_reduce(top[:, :], stats[:, :], P, RMAX).then_inc(top_ready, 1)
            steps = 1
            while half > 1:
                half //= 2
                pool.wait_ge(tree_step, steps)
                ins = nc.gpsimd.tensor_tensor(tree[:, 0:half, :], tree[:, 0:half, :], tree[:, half:2 * half, :],
                                              ALU.add)
                ins.then_inc(tree_step if half > 1 else tree_ready, 1)
                steps += 1
            for half, w in ((0, 0), (0, 1), (1, 0)):
                if half == 1:
                    pool.wait_ge(g32_ready[0], 2)
                    nc.gpsimd.tensor_tensor(g32[:, 1, HALF:NB, 0:D], xs[:, HALF:NB, :],
                                            e12[:, 1, HALF:NB].unsqueeze(2).to_broadcast([P, HALF, D]),
                                            ALU.mult).then_inc(g32_by_pool, 1)
                pool.wait_ge(ghi_ready[half], w + 1)
                bs = slice(half * HALF, (half + 1) * HALF)
                nc.gpsimd.tensor_tensor(g[:, w, bs, 1, :], g32[:, w, bs, :], g[:, w, bs, 0, :],
                                        ALU.subtract).then_inc(glo_ready[half], 1)
            pool.wait_ge(mean_ready, 1)

            def deviation(c, link):
                pool.wait_ge(vsum_ready, c + 1)
                link(nc.gpsimd.tensor_tensor(vmean[:, :], vsum[:, :], inv_d[:, :], ALU.mult))
                link(nc.gpsimd.tensor_tensor(var[:, :], vmean[:, :], eps[:, :], ALU.add))
                nc.gpsimd.tensor_tensor(rstd[:, :], var[:, :], neg_half[:, :], ALU.pow).then_inc(rstd_ready, 1)
                pool.wait_ge(rstd_ready, c + 1)

            def chunk(c, first=False):
                chain = [0]

                def link(ins):
                    chain[0] += 1
                    ins.then_inc(rows_step, 1)
                    pool.wait_ge(rows_step, c * ROWS_STEPS + chain[0])

                pool.wait_ge(sums_taken, c * T + 2 * T)
                link(nc.gpsimd.tensor_tensor(both[:, :, 0, :], both[:, :, 0, :], both[:, :, 1, :], ALU.add))
                nc.gpsimd.tensor_tensor(total[:, :, :], both[:, :, 0, 0:W], both[:, :, 0, W:2 * W],
                                        ALU.add).then_inc(total_ready, 1)
                rows_out(pool, nc.gpsimd, c, link)
                centre(pool, nc.gpsimd, c, link)
                deviation(c, link)
                if not first:
                    pool.wait_ge(res_stored, c * 16)
                link(nc.gpsimd.tensor_tensor(res[:, :, :], zc[:, :, :],
                                             rstd[:, :].unsqueeze(2).to_broadcast([P, T, D]), ALU.mult))
                pool.dma_start(out_b[:, bass.ds(c * (T // 2), T // 2)], pairs(res)).then_inc(res_stored, 16)
                assert chain[0] == ROWS_STEPS

            chunk(0, first=True)
            with pool.Fori(1, C - 1) as c:
                chunk(c)
            for t in range(T):
                pool.wait_ge(last_var_ready, t + 1)
                nc.gpsimd.tensor_tensor(last_rstd[:, t:t + 1], last_var[:, t:t + 1], neg_half[:, t:t + 1],
                                        ALU.pow).then_inc(last_rstd_ready, 1)
            pool.wait_ge(res_stored, (C - 1) * 16)


def kernel(x, adj, L0_gnn_a):
    import numpy as _np
    import concourse.bacc as _bacc
    from concourse import mybir as _mybir
    from concourse.bass_utils import run_bass_kernel_spmd as _run

    nc = _bacc.Bacc("TRN2", target_bir_lowering=False, num_devices=1)
    arrays, args = {}, []
    for name, value in (("x", x), ("adj", adj), ("a", L0_gnn_a)):
        value = _np.ascontiguousarray(value)
        arrays[f"in_{name}"] = value
        args.append(nc.dram_tensor(f"in_{name}", value.shape, _mybir.dt.from_np(value.dtype),
                                   kind="ExternalInput").ap())
    out = nc.dram_tensor("out_0", tuple(x.shape), _mybir.dt.float32, kind="ExternalOutput").ap()
    gat_layernorm(nc, *args, out)
    result = _run(nc, [arrays], core_ids=[0])
    return result.results[0]["out_0"]
```

```python
from contextlib import ExitStack

import concourse.bass as bass
from concourse import mybir
import numpy as np

ALU = mybir.AluOpType
ACT = mybir.ActivationFunctionType
AX_X = mybir.AxisListType.X
F32 = mybir.dt.float32
F16 = mybir.dt.float16
BF16 = mybir.dt.bfloat16
FP8 = mybir.dt.float8e4
I32 = mybir.dt.int32
RMAX = bass.bass_isa.ReduceOp.max

P = 128
SLOPE = 0.01
NEG_INF = -9000000000000000.0
EPS = 1e-5

ABOVE = 1.0
ABOVE_BYTE = 1.875
BELOW = float(np.array([0x00B80000], np.uint32).view(np.float32)[0])
BELOW_BYTE = -1.0

G_SCALE = 2048.0
MAX_SPREAD = 9.0
MIN_X, MAX_X = 0.5, 16.0
MAX_A = 1024.0
MAX_TOP = 60.0


def gat_layernorm(nc, x, adj, a, out):
    N, D = x.shape
    NB = N // P
    T = 4
    C = NB // T
    H = 2
    UW = N // H
    UB = UW // P
    U = T * H
    W = D + 1
    BANK = 512
    Q = 4
    HALF = NB // 2

    x_b = x.rearrange("(g p q) d -> p g q d", p=P, q=2)
    out_b = out.rearrange("(g p q) d -> p g q d", p=P, q=2)
    adj_b = adj.rearrange("(g p q) j -> g q p j", p=P, q=2)
    a_row = a.rearrange("(a n) o -> o a n", a=2)
    a_col = a.rearrange("(a n) o -> n (a o)", a=2)

    with ExitStack() as ctx:
        def sb(name, shape, dt):
            return ctx.enter_context(nc.sbuf_tensor(name, shape, dt))

        def pb(name, shape, dt):
            return ctx.enter_context(nc.psum_tensor(name, shape, dt))

        def sem(name):
            return ctx.enter_context(nc.semaphore(name))

        CLEANS, THRS, CODES, TURNED = 4, 4, 2, 2
        ring = sb("ring", [P, U, UW], I32)
        clean = sb("clean", [P, CLEANS, UW], BF16)
        thr = sb("thr", [P, THRS, UW], BF16)
        code = sb("code", [P, CODES, UW], BF16)
        turned = sb("turned", [P, TURNED, UW], BF16)
        ident = sb("ident", [P, P], F32)
        ident16 = sb("ident16", [P, P], BF16)
        ident16h = sb("ident16h", [P, P], F16)
        ones = sb("ones", [P, P], F32)
        eps = sb("eps", [P, T], F32)
        inv_d = sb("inv_d", [P, T], F32)
        neg_half = sb("neg_half", [P, T], F32)
        xs = sb("xs", [P, NB, D], F32)
        d_all = sb("d_all", [P, N], F32)
        g = sb("g", [P, 2, NB, 2, W], F16)
        ns = sb("ns", [P, NB], F32)
        ratio = sb("ratio", [P, NB, 2], F32)
        mean_row = sb("mean_row", [P, D], F32)
        flag = sb("flag", [P, 1], I32)
        x16 = sb("x16", [P, NB, 2, D], F16)
        xt16 = sb("xt16", [P, N], F16)
        g32 = sb("g32", [P, 2, NB, W], F32)
        tree = sb("tree", [P, NB // 2, D], F32)
        a_rows = sb("a_rows", [P, 2, D], F32)
        a_cols = sb("a_cols", [P, 2], F32)
        a16 = sb("a16", [P, 2, 2], F16)
        a_rep = sb("a_rep", [P, 2, P], F16)
        sd = sb("sd", [P, 2, NB], F32)
        stats = sb("stats", [P, 5], F32)
        top = sb("top", [P, 5], F32)
        bias = sb("bias", [P, 2], F32)
        within = sb("within", [P, 7], F32)
        e12 = sb("e12", [P, 2, NB], F32)
        u = sb("u", [P, NB], F32)
        f = sb("f", [P, NB], F32)
        both = sb("both", [P, T, 2, 2 * W], F32)
        total = sb("total", [P, T, W], F32)
        empty = sb("empty", [P, T], F32)
        den = sb("den", [P, T], F32)
        rden = sb("rden", [P, T], F32)
        fill = sb("fill", [P, T, D], F32)
        full = sb("full", [P, T, D], F32)
        att = sb("att", [P, T, D], F32)
        z = sb("z", [P, T, D], F32)
        zsum = sb("zsum", [P, T], F32)
        mean = sb("mean", [P, T], F32)
        zc = sb("zc", [P, T, D], F32)
        sq = sb("sq", [P, T, D], F32)
        vsum = sb("vsum", [P, T], F32)
        vmean = sb("vmean", [P, T], F32)
        var = sb("var", [P, T], F32)
        rstd = sb("rstd", [P, T], F32)
        res = sb("res", [P, T, D], F32)
        spare = x16.rearrange("p b h d -> p (b h d)").bitcast(F32)
        last_total = spare[:, 0:T * W].rearrange("p (t w) -> p t w", t=T)
        last_base, last_z, last_res = (
            spare[:, T * (W + k * D):T * (W + (k + 1) * D)].rearrange("p (t d) -> p t d", t=T) for k in range(3))
        last_empty = sb("last_empty", [P, T], F32)
        last_den = sb("last_den", [P, T], F32)
        last_rden = sb("last_rden", [P, T], F32)
        last_stats = sb("last_stats", [P, T, 6], F32)
        last_mean_var = sb("last_mean_var", [P, T, 2], F32)
        last_var = sb("last_var", [P, T], F32)
        last_rstd = sb("last_rstd", [P, T], F32)
        gadj, ge, gt = (ring[:, k * H:(k + 1) * H, :].rearrange("p h w -> p (h w)") for k in range(3))
        ge, gt = ge.bitcast(F32), gt.bitcast(F32)
        gv = sb("gv", [P, 10], F32)
        gxt = gt[0:D, 0:BANK]
        gen_rep = gt[0:D, BANK:BANK + P]
        gx = att[:, 0, :]
        gy = sq

        pt = pb("pt", [P, 2, UW], BF16)
        acc = pb("acc", [P, T, BANK], F32)

        def words(ap):
            return ap.bitcast(F32)

        def rows_of(ap, b):
            return ap[:, (b // 2) * 2 * P:(b // 2 + 1) * 2 * P].rearrange("p (i q) -> p q i", q=2)[:, b % 2, :]

        def early_bank(k):
            return acc[:, k, :] if k < T else pt[:, (k - T) // 2, :].bitcast(F32)[:, (k % 2) * BANK:(k % 2 + 1) * BANK]

        x_loaded = [sem(f"x_loaded{q}") for q in range(Q)]
        a_loaded = sem("a_loaded")
        zeroed = sem("zeroed")
        x_high = sem("x_high")
        x_low = [sem(f"x_low{q}") for q in range(Q)]
        a16_step = sem("a16_step")
        a_rep_ready = sem("a_rep_ready")
        x_transposed = sem("x_transposed")
        xt_copied = sem("xt_copied")
        sd_summed = sem("sd_summed")
        sd_ready = sem("sd_ready")
        ns_ready = sem("ns_ready")
        consts_ready = sem("consts_ready")
        d_summed = sem("d_summed")
        d_copied = sem("d_copied")
        stats_ready = sem("stats_ready")
        top_ready = sem("top_ready")
        bias_ready = sem("bias_ready")
        e_ready = sem("e_ready")
        e_scaled = sem("e_scaled")
        g32_ready = [sem(f"g32_ready{half}") for half in range(2)]
        g32_by_pool = sem("g32_by_pool")
        ghi_ready = [sem(f"ghi_ready{half}") for half in range(2)]
        glo_ready = [sem(f"glo_ready{half}") for half in range(2)]
        flag_step = sem("flag_step")
        flag_ready = sem("flag_ready")
        u_ready = sem("u_ready")
        f_ready = sem("f_ready")
        ratio_ready = sem("ratio_ready")
        tree_step = sem("tree_step")
        tree_ready = sem("tree_ready")
        mean_summed = sem("mean_summed")
        mean_ready = sem("mean_ready")
        unit_loaded = [sem(f"unit_loaded{m}") for m in range(U)]
        clean_ready = sem("clean_ready")
        thr_ready = sem("thr_ready")
        code_ready = sem("code_ready")
        transposed = sem("transposed")
        turned_ready = sem("turned_ready")
        products_done = sem("products_done")
        sums_taken = sem("sums_taken")
        total_ready = sem("total_ready")
        den_step = sem("den_step")
        rden_ready = sem("rden_ready")
        rows_step = sem("rows_step")
        z_ready = sem("z_ready")
        zsum_ready = sem("zsum_ready")
        sq_ready = sem("sq_ready")
        vsum_ready = sem("vsum_ready")
        rstd_ready = sem("rstd_ready")
        res_stored = sem("res_stored")
        last_step = sem("last_step")
        last_var_ready = sem("last_var_ready")
        last_rstd_ready = sem("last_rstd_ready")
        last_res_ready = sem("last_res_ready")
        last_stored = sem("last_stored")
        gen_ready = sem("gen_ready")
        gen_xt = sem("gen_xt")
        gen_d = sem("gen_d")
        gen_loaded = sem("gen_loaded")
        gen_step = sem("gen_step")
        gen_masked = sem("gen_masked")
        gen_weights = sem("gen_weights")
        gen_turned = sem("gen_turned")
        gen_copied = sem("gen_copied")
        gen_summed = sem("gen_summed")
        gen_var = sem("gen_var")
        gen_dev = sem("gen_dev")
        gen_res = sem("gen_res")
        gen_stored = sem("gen_stored")

        block = ctx.enter_context(nc.Block())

        def general(eng):
            eng.wait_ge(flag_ready, 1)
            return eng.If(eng.value_load(flag[0:1, 0:1], min_val=0, max_val=1) > 0)

        def unit(c, m):
            return (c, m) if m < U else (c + 1, m - U)

        def at(c, m, back=0):
            n = c * U + (m + 1 - back)
            return None if isinstance(n, int) and n < 1 else n

        EARLY = list(range(T - 1))

        def pairs(ap):
            return ap.rearrange("p (g q) d -> p g q d", q=2)

        def tile_rows(c, t):
            return adj_b[c * (T // 2) + t // 2, t % 2]

        def tile(c, t):
            n = c * T + t
            return slice(n, n + 1) if isinstance(n, int) else bass.ds(n, 1)

        @block.sync
        def _(sp):
            bq = NB // Q
            for q in range(Q):
                sp.dma_start(pairs(xs)[:, q * bq // 2:(q + 1) * bq // 2], x_b[:, q * bq // 2:(q + 1) * bq // 2])\
                    .then_inc(x_loaded[q], 16)

            def load(c, m):
                sp.dma_start(ring[:, m, :], tile_rows(c, m // H)[:, (m % H) * UW:(m % H + 1) * UW])\
                    .then_inc(unit_loaded[m], 16)

            for m in range(U):
                load(0, m)
            with sp.Fori(1, C) as c:
                for m in range(U):
                    sp.wait_ge(clean_ready, c * U + (m + 1 - U))
                    load(c, m)
            sp.wait_ge(last_res_ready, T)
            sp.dma_start(out_b[:, (C - 1) * (T // 2):C * (T // 2)], pairs(last_res)).then_inc(last_stored, 16)
            sp.wait_ge(last_stored, 16)
            with general(sp):
                sp.wait_ge(res_stored, (C - 1) * 16)

                def load_tile(k):
                    sp.dma_start(gadj, adj.rearrange("(k p) j -> k p j", p=P)[k]).then_inc(gen_loaded, 16)
                    sp.dma_start(gx, x.rearrange("(k p) d -> k p d", p=P)[k]).then_inc(gen_loaded, 16)

                def store_tile(k):
                    sp.wait_ge(gen_res, k + 1)
                    sp.dma_start(out.rearrange("(k p) d -> k p d", p=P)[k], gy[:, 3, :]).then_inc(gen_stored, 16)
                    sp.wait_ge(gen_stored, (k + 1) * 16)

                load_tile(0)
                with sp.Fori(0, NB - 1) as k:
                    store_tile(k)
                    load_tile(k + 1)
                store_tile(NB - 1)

        @block.tensor
        def _(pe):
            def products_wait(c, m):
                pe.wait_ge(turned_ready, at(c, m))
                if m % H == 0:
                    pe.wait_ge(sums_taken, c * T + (m // H + 1))

            def transposes(c, m, then=None):
                c, m = unit(c, m)
                pe.wait_ge(code_ready, at(c, m))
                if at(c, m, 2) is not None:
                    pe.wait_ge(turned_ready, at(c, m, 2))
                for b in range(UB):
                    if then and b == UB - 1:
                        products_wait(*unit(*then))
                    last = nc.tensor.transpose(pt[:, m % 2, b * P:(b + 1) * P],
                                               rows_of(code[:, m % CODES, :], b), ident16[:, :])
                last.then_inc(transposed, 1)

            def products(c, m):
                t = m // H
                for b in range(UB):
                    blk = (m % H) * UB + b
                    planes = turned[:, m % TURNED, b * P:(b + 1) * P].bitcast(FP8).rearrange("p (i h) -> p h i", h=2)
                    nc.tensor.matmul(acc[:, t, 0:2 * W], planes[:, 1, :],
                                     g[:, 0, blk, :, :].rearrange("p h w -> p (h w)"),
                                     start=(blk == 0), stop=(blk == NB - 1), skip_group_check=True)
                    last = nc.tensor.matmul(acc[:, t, 2 * W:4 * W], planes[:, 0, :],
                                            g[:, 1, blk, :, :].rearrange("p h w -> p (h w)"),
                                            start=False, stop=(blk == NB - 1), skip_group_check=True)
                last.then_inc(products_done, 1)

            pe.wait_ge(consts_ready, 8)
            for q in range(Q):
                pe.wait_ge(x_high, q + 1)
                pe.wait_ge(x_low[q], 1)
                for b in range(NB // Q):
                    last = nc.tensor.transpose(early_bank(q).bitcast(F16)[:, b * P:(b + 1) * P],
                                               x16[:, q * (NB // Q) + b, :, :].rearrange("p h d -> p (h d)"),
                                               ident16h[:, :])
                last.then_inc(x_transposed, 1)
            pe.wait_ge(a_rep_ready, 2)
            for q in range(Q):
                pe.wait_ge(xt_copied, q + 1)
                for b in range(q * NB // Q, (q + 1) * NB // Q):
                    last = nc.tensor.matmul(early_bank(7)[:, 4 * b:4 * b + 4], xt16[:, b * P:(b + 1) * P],
                                            a16[:, :, :].rearrange("p h a -> p (h a)"), start=True, stop=True)
            last.then_inc(sd_summed, 1)
            in_order = xt16.rearrange("p (g q i) -> p g i q", q=2, i=P)
            for k in range(N // BANK):
                if k >= 3:
                    pe.wait_ge(d_copied, k - 2)
                for h in range(2):
                    last = nc.tensor.matmul(early_bank(T + k % 3), a_rep[:, h, :], in_order[:, 2 * k:2 * k + 2],
                                            start=(h == 0), stop=(h == 1))
                last.then_inc(d_summed, 1)
            pe.wait_ge(tree_ready, 1)
            nc.tensor.matmul(early_bank(T - 1)[:, 0:D], ones[:, :], tree[:, 0, :], start=True, stop=True)\
                .then_inc(mean_summed, 1)
            pe.wait_ge(d_copied, N // BANK)
            pe.wait_ge(sd_ready, 1)
            pe.wait_ge(mean_ready, 1)
            transposes(0, 0)
            transposes(0, 1)
            for m in range(H):
                pe.wait_ge(glo_ready[m], 2)
                products_wait(0, m)
                products(0, m)
            transposes(0, 2)
            transposes(0, 3, (0, 2))
            for m in range(2, U):
                products(0, m)
                transposes(0, m + 2, (0, m + 1))

            with pe.Fori(1, C - 1) as c:
                for m in range(U):
                    products(c, m)
                    transposes(c, m + 2, (c, m + 1))
            for m in range(U):
                products(C - 1, m)
                if m + 2 < U:
                    transposes(C - 1, m + 2, (C - 1, m + 1))
                elif m + 1 < U:
                    products_wait(C - 1, m + 1)

            with general(pe):
                pe.wait_ge(gen_ready, 1)
                for k in range(N // BANK):
                    if k >= 1:
                        pe.wait_ge(gen_d, 2 * k)
                    for b in range(4):
                        last = nc.tensor.transpose(rows_of(early_bank(T)[0:D, :], b), xs[:, 4 * k + b, :],
                                                   ident[:, :])
                    last.then_inc(gen_xt, 1)
                    pe.wait_ge(gen_d, 2 * k + 1)
                    nc.tensor.matmul(early_bank(T + 2), gen_rep[:, :], gxt[:, :], start=True, stop=True)\
                        .then_inc(gen_xt, 1)
                pe.wait_ge(gen_d, 2 * (N // BANK))
                with pe.Fori(0, NB) as k:
                    pe.wait_ge(gen_weights, k + 1)
                    for h in range(4):
                        if h >= 1:
                            pe.wait_ge(gen_copied, k * 4 + h)
                        for b in range(8):
                            last = nc.tensor.transpose(early_bank(T + b // 4)[:, (b % 4) * P:(b % 4 + 1) * P],
                                                       rows_of(ge, h * 8 + b), ident[:, :])
                        last.then_inc(gen_turned, 1)
                    pe.wait_ge(gen_copied, k * 4 + 4)
                    for b in range(NB):
                        last = nc.tensor.matmul(acc[:, 0, 0:D], gt[:, b * P:(b + 1) * P], xs[:, b, :],
                                                start=(b == 0), stop=(b == NB - 1))
                    last.then_inc(gen_summed, 1)

        @block.scalar
        def _(act):
            with nc.allow_non_contiguous_dma(reason="256 bytes of a"):
                act.dma_start(a_cols[0:D, :], a_col).then_inc(a_loaded, 16)
            with nc.allow_non_contiguous_dma(reason="256 bytes of a"):
                act.dma_start(a_cols[D:P, :], a_col).then_inc(a_loaded, 16)
            act.dma_start(a_rows[:, :, :], a_row.to_broadcast([P, 2, D])).then_inc(a_loaded, 16)

            def clean_adj(c, m):
                c, m = unit(c, m)
                act.wait_ge(unit_loaded[m], (c + 1) * 16)
                if at(c, m, CLEANS) is not None:
                    act.wait_ge(code_ready, at(c, m, CLEANS))
                nc.scalar.activation(clean[:, m % CLEANS, :], ring[:, m, :], ACT.Relu).then_inc(clean_ready, 1)

            AHEAD = 3

            def turn(c, m):
                act.wait_ge(transposed, at(c, m))
                if at(c, m, TURNED) is not None:
                    act.wait_ge(products_done, at(c, m, TURNED))
                nc.scalar.copy(words(turned[:, m % TURNED, :]), words(pt[:, m % 2, :])).then_inc(turned_ready, 1)

            for q in range(Q):
                act.wait_ge(x_transposed, q + 1)
                nc.scalar.copy(words(xt16[:, q * (N // Q):(q + 1) * (N // Q)]), early_bank(q)).then_inc(xt_copied, 1)

            def copy_d(k):
                act.wait_ge(d_summed, k + 1)
                nc.scalar.copy(d_all[:, k * BANK:(k + 1) * BANK], early_bank(T + k % 3)).then_inc(d_copied, 1)

            for k in range(2):
                copy_d(k)
            act.wait_ge(bias_ready, 2)
            nc.scalar.activation(e12[:, 0, :], sd[:, 1, :], ACT.Exp, bias=bias[:, 0:1], scale=1.0)\
                .then_inc(e_ready, 1)
            nc.scalar.activation(e12[:, 1, :], sd[:, 1, :], ACT.Exp, bias=bias[:, 1:2], scale=SLOPE)\
                .then_inc(e_ready, 1)
            for k in range(2, N // BANK):
                copy_d(k)
                if k == N // BANK // 2 - 1:
                    clean_adj(0, 0)
            clean_adj(0, 1)
            act.wait_ge(u_ready, 1)
            nc.scalar.activation(f[:, :], u[:, :], ACT.Exp, scale=1.0 - SLOPE).then_inc(f_ready, 1)
            act.wait_ge(f_ready, 1)
            nc.scalar.mul(ratio[:, :, 0], f[:, :], BELOW_BYTE / ABOVE_BYTE).then_inc(ratio_ready, 1)
            act.wait_ge(mean_summed, 1)
            nc.scalar.mul(mean_row[:, :], early_bank(T - 1)[:, 0:D], 1.0 / N).then_inc(mean_ready, 1)
            for m in range(H, AHEAD):
                clean_adj(0, m)

            def chunk(c, last=False):
                for m in range(U):
                    turn(c, m)
                    if not last:
                        clean_adj(c, m + AHEAD)
                    elif AHEAD - 2 <= m < U - 2:
                        clean_adj(c, m + 2)

            chunk(0)
            with act.Fori(1, C - 1) as c:
                chunk(c)
            chunk(C - 1, last=True)

            with general(act):
                with act.Fori(0, NB) as k:
                    act.wait_ge(gen_masked, k + 1)
                    nc.scalar.activation(ge, ge, ACT.Exp, bias=gv[:, 2:3], scale=1.0,
                                         accum_out=gv[:, 3:4]).then_inc(gen_weights, 1)
                    act.wait_ge(gen_var, k + 1)
                    nc.scalar.activation(gv[:, 8:9], gv[:, 7:8], ACT.Sqrt).then_inc(gen_dev, 1)

        @block.vector
        def _(dve):
            def threshold(c, m):
                c, m = unit(c, m)
                if at(c, m, THRS) is not None:
                    dve.wait_ge(code_ready, at(c, m, THRS))
                nc.vector.tensor_scalar(thr[:, m % THRS, :], d_all[:, (m % H) * UW:(m % H + 1) * UW],
                                        ns[:, tile(c, m // H)], BELOW, ALU.is_gt, ALU.max).then_inc(thr_ready, 1)

            def combine(c, m):
                dve.wait_ge(thr_ready, at(c, m))
                dve.wait_ge(clean_ready, at(c, m))
                if at(c, m, CODES) is not None:
                    dve.wait_ge(transposed, at(c, m, CODES))
                nc.vector.tensor_tensor(code[:, m % CODES, :], clean[:, m % CLEANS, :], thr[:, m % THRS, :],
                                        ALU.min).then_inc(code_ready, 1)

            def take_sums(c, t):
                dve.wait_ge(products_done, at(c, t * H + H - 1))
                if t == 0 and not (isinstance(c, int) and c == 0):
                    dve.wait_ge(total_ready, c)
                nc.vector.tensor_tensor(both[:, t, :, :],
                                        acc[:, t, 0:4 * W].rearrange("p (w k) -> p w k", w=2),
                                        ratio[:, tile(c, t), :].rearrange("p o w -> p (o w)").unsqueeze(2)
                                        .to_broadcast([P, 2, 2 * W]), ALU.mult).then_inc(sums_taken, 1)

            def recip_den(c):
                dve.wait_ge(total_ready, c + 1)
                nc.vector.tensor_scalar(empty[:, :], total[:, :, D], 0.0, None, ALU.is_equal).then_inc(den_step, 1)
                dve.wait_ge(den_step, c * 2 + 1)
                nc.vector.tensor_tensor(den[:, :], empty[:, :], total[:, :, D], ALU.add).then_inc(den_step, 1)
                dve.wait_ge(den_step, c * 2 + 2)
                nc.vector.reciprocal(rden[:, :], den[:, :]).then_inc(rden_ready, 1)

            def sum_z(c):
                dve.wait_ge(z_ready, c + 1)
                nc.vector.tensor_reduce(zsum[:, :], z[:, :, :], AX_X, ALU.add).then_inc(zsum_ready, 1)

            def sum_sq(c):
                dve.wait_ge(sq_ready, c + 1)
                nc.vector.tensor_reduce(vsum[:, :], sq[:, :, :], AX_X, ALU.add).then_inc(vsum_ready, 1)

            dve.sem_inc(sums_taken, T)
            for q in range(Q):
                dve.wait_ge(x_loaded[q], 16)
                bs = slice(q * (NB // Q), (q + 1) * (NB // Q))
                nc.vector.tensor_copy(x16[:, bs, 0, :], xs[:, bs, :]).then_inc(x_high, 1)
                if q == 1:
                    dve.wait_ge(a_loaded, 48)
                    nc.vector.tensor_copy(a16[:, 0, :], a_cols[:, :]).then_inc(a16_step, 1)
                    dve.wait_ge(a16_step, 1)
                    nc.vector.tensor_tensor(a16[:, 1, :], a_cols[:, :], a16[:, 0, :],
                                            ALU.subtract).then_inc(a16_step, 1)
                    dve.wait_ge(a16_step, 2)
                    for h in range(2):
                        nc.vector.tensor_copy(a_rep[:, h, :],
                                              a16[:, h, 1:2].to_broadcast([P, P])).then_inc(a_rep_ready, 1)
                if q % 2 == 1:
                    dve.wait_ge(x_high, q + 1)
                    nc.vector.tensor_tensor(x16[:, bs, 1, :], xs[:, bs, :], x16[:, bs, 0, :],
                                            ALU.subtract).then_inc(x_low[q], 1)
            nc.vector.tensor_reduce(stats[:, 2:3], xs[:, :, :], mybir.AxisListType.XY, ALU.max,
                                    apply_absolute_value=True)
            nc.vector.tensor_reduce(stats[:, 4:5], a_cols[:, :], AX_X, ALU.max, apply_absolute_value=True)
            dve.wait_ge(sd_summed, 1)
            nc.vector.tensor_reduce(sd[:, :, :],
                                    early_bank(7)[:, 0:4 * NB].rearrange("p (b h a) -> p a b h", h=2, a=2),
                                    AX_X, ALU.add).then_inc(sd_ready, 1)
            dve.wait_ge(sd_ready, 1)
            nc.vector.tensor_reduce(stats[:, 0:1], sd[:, 1, :], AX_X, ALU.max)
            nc.vector.tensor_reduce(stats[:, 3:4], sd[:, 0, :], AX_X, ALU.max)
            nc.vector.tensor_reduce(stats[:, 1:2], sd[:, 1, :], AX_X, ALU.min, negate=True).then_inc(stats_ready, 1)
            nc.vector.tensor_scalar(ns[:, :], sd[:, 0, :], -1.0, None, ALU.mult).then_inc(ns_ready, 1)
            dve.wait_ge(top_ready, 1)
            nc.vector.tensor_scalar(bias[:, 0:1], top[:, 0:1], -1.0, None, ALU.mult).then_inc(bias_ready, 1)
            nc.vector.tensor_scalar(bias[:, 1:2], top[:, 0:1], -SLOPE, None, ALU.mult).then_inc(bias_ready, 1)
            nc.vector.tensor_scalar(u[:, :], sd[:, 0, :], top[:, 0:1], MAX_TOP, ALU.add, ALU.min).then_inc(u_ready, 1)
            dve.wait_ge(e_ready, 2)
            nc.vector.tensor_scalar(e12[:, :, :], e12[:, :, :], G_SCALE, None, ALU.mult).then_inc(e_scaled, 1)
            dve.wait_ge(e_scaled, 1)
            nc.vector.tensor_copy(g32[:, :, :, D], e12[:, :, :]).then_inc(e_scaled, 1)

            def scale_x(w, half):
                bs = slice(half * HALF, (half + 1) * HALF)
                nc.vector.tensor_tensor(g32[:, w, bs, 0:D], xs[:, bs, :],
                                        e12[:, w, bs].unsqueeze(2).to_broadcast([P, HALF, D]),
                                        ALU.mult).then_inc(g32_ready[half], 1)

            def high_part(w, half):
                bs = slice(half * HALF, (half + 1) * HALF)
                if (w, half) == (1, 1):
                    dve.wait_ge(g32_by_pool, 1)
                else:
                    dve.wait_ge(g32_ready[half], w + 1)
                nc.vector.tensor_copy(g[:, w, bs, 0, :], g32[:, w, bs, :]).then_inc(ghi_ready[half], 1)

            for w in range(2):
                scale_x(w, 0)
            dve.wait_ge(e_scaled, 2)
            for w in range(2):
                high_part(w, 0)
            dve.wait_ge(ns_ready, 1)
            for m in range(H):
                dve.wait_ge(d_copied, (m + 1) * (N // BANK) // H)
                threshold(0, m)
                combine(0, m)
            scale_x(0, 1)
            high_part(0, 1)
            high_part(1, 1)
            dve.wait_ge(ghi_ready[1], 2)
            nc.vector.tensor_tensor(g[:, 1, HALF:NB, 1, :], g32[:, 1, HALF:NB, :], g[:, 1, HALF:NB, 0, :],
                                    ALU.subtract).then_inc(glo_ready[1], 1)
            dve.wait_ge(ratio_ready, 1)

            def raise_flag():
                nc.vector.tensor_scalar(within[:, 0:1], top[:, 0:1], top[:, 1:2], MAX_SPREAD, ALU.add,
                                        ALU.is_le).then_inc(flag_step, 1)
                nc.vector.tensor_scalar(within[:, 1:2], top[:, 2:3], MIN_X, None, ALU.is_ge).then_inc(flag_step, 1)
                nc.vector.tensor_scalar(within[:, 2:3], top[:, 0:1], top[:, 3:4], MAX_TOP, ALU.add,
                                        ALU.is_le).then_inc(flag_step, 1)
                dve.wait_ge(flag_step, 3)
                nc.vector.scalar_tensor_tensor(out=within[:, 3:4], in0=top[:, 4:5], scalar=MAX_A,
                                               in1=within[:, 0:1], op0=ALU.is_le,
                                               op1=ALU.mult).then_inc(flag_step, 1)
                nc.vector.scalar_tensor_tensor(out=within[:, 4:5], in0=top[:, 2:3], scalar=MAX_X,
                                               in1=within[:, 1:2], op0=ALU.is_le,
                                               op1=ALU.mult).then_inc(flag_step, 1)
                dve.wait_ge(flag_step, 5)
                nc.vector.tensor_tensor(within[:, 5:6], within[:, 3:4], within[:, 4:5],
                                        ALU.mult).then_inc(flag_step, 1)
                dve.wait_ge(flag_step, 6)
                nc.vector.tensor_tensor(within[:, 6:7], within[:, 2:3], within[:, 5:6],
                                        ALU.mult).then_inc(flag_step, 1)
                dve.wait_ge(flag_step, 7)
                nc.vector.tensor_scalar(flag[:, :], within[:, 6:7], -1.0, 1.0, ALU.mult,
                                        ALU.add).then_inc(flag_ready, 1)

            def chunk(c, first=False, last=False):
                for m in range(U):
                    if not (first and m < 2):
                        combine(c, m)
                    if not (last and m + 2 >= U):
                        threshold(c, m + 2)
                    if m in (1, 3) and not first:
                        take_sums(c - 1, T - 2 + m // 2)
                    if not first:
                        if m == 4:
                            recip_den(c - 1)
                        if m == 6:
                            sum_z(c - 1)
                        if m == 7:
                            sum_sq(c - 1)
                    elif m == 3:
                        raise_flag()
                    if m in (5, 7):
                        take_sums(c, m // 2 - 2)

            done = [0]

            def last_rows(tiles):
                def step(operation, first=False, signal=last_step):
                    for k, t in enumerate(tiles):
                        if not first:
                            dve.wait_ge(last_step, done[0] + k + 1 - len(tiles))
                        operation(t, slice(t, t + 1)).then_inc(signal, 1)
                    done[0] += len(tiles)

                dve.wait_ge(sums_taken, T + (C - 1) * T + tiles[-1] + 1)
                step(lambda t, one: nc.vector.tensor_reduce(
                    last_total[:, t, :], both[:, t, :, :].rearrange("p w (h k) -> p k w h", h=2),
                    mybir.AxisListType.XY, ALU.add), first=True)
                step(lambda t, one: nc.vector.tensor_scalar(
                    last_empty[:, one], last_total[:, t, D:W], 0.0, None, ALU.is_equal))
                step(lambda t, one: nc.vector.tensor_tensor(
                    last_den[:, one], last_total[:, t, D:W], last_empty[:, one], ALU.add))
                step(lambda t, one: nc.vector.reciprocal(last_rden[:, one], last_den[:, one]))
                step(lambda t, one: nc.vector.scalar_tensor_tensor(
                    out=last_base[:, t, :], in0=mean_row[:, :], scalar=last_empty[:, one],
                    in1=xs[:, (C - 1) * T + t, :], op0=ALU.mult, op1=ALU.add))
                step(lambda t, one: nc.vector.scalar_tensor_tensor(
                    out=last_z[:, t, :], in0=last_total[:, t, 0:D], scalar=last_rden[:, one],
                    in1=last_base[:, t, :], op0=ALU.mult, op1=ALU.add))
                step(lambda t, one: nc.vector.bn_stats(last_stats[:, t, :], last_z[:, t, :]))
                step(lambda t, one: nc.vector.bn_aggr(last_mean_var[:, t, :], last_stats[:, t, :]))
                step(lambda t, one: nc.vector.tensor_scalar(
                    last_var[:, one], last_mean_var[:, t, 1:2], EPS, None, ALU.add), signal=last_var_ready)
                done[0] -= len(tiles)

            def last_scale(t):
                dve.wait_ge(last_rstd_ready, 1 if t in EARLY else 2)
                nc.vector.tensor_scalar(last_res[:, t, :], last_z[:, t, :], last_mean_var[:, t, 0:1],
                                        last_rstd[:, t:t + 1], ALU.subtract, ALU.mult).then_inc(last_res_ready, 1)

            chunk(0, first=True)
            with dve.Fori(1, C - 1) as c:
                chunk(c)
            chunk(C - 1, last=True)
            take_sums(C - 1, 2)
            last_rows(EARLY)
            take_sums(C - 1, 3)
            last_rows([T - 1])
            for t in range(T):
                last_scale(t)

            with general(dve):
                dve.wait_ge(clean_ready, C * U)
                nc.vector.tensor_copy(gen_rep, a_cols[0:D, 1:2].to_broadcast([D, P])).then_inc(gen_ready, 1)
                for k in range(N // BANK):
                    dve.wait_ge(gen_xt, 2 * k + 1)
                    nc.vector.tensor_copy(gxt, early_bank(T)[0:D, :]).then_inc(gen_d, 1)
                    dve.wait_ge(gen_xt, 2 * k + 2)
                    nc.vector.tensor_copy(d_all[:, k * BANK:(k + 1) * BANK], early_bank(T + 2)).then_inc(gen_d, 1)
                dve.wait_ge(gen_d, 2 * (N // BANK))
                STEPS = 16
                with dve.Fori(0, NB) as k:
                    chain = [0]

                    def glink(ins):
                        chain[0] += 1
                        ins.then_inc(gen_step, 1)
                        dve.wait_ge(gen_step, k * STEPS + chain[0])

                    dve.wait_ge(gen_loaded, (k + 1) * 32)
                    glink(nc.vector.tensor_tensor(gy[:, 0, :], gx, a_rows[:, 0, :], ALU.mult))
                    glink(nc.vector.tensor_reduce(gv[:, 0:1], gy[:, 0, :], AX_X, ALU.add))
                    glink(nc.vector.tensor_scalar(gt, d_all[:, :], gv[:, 0:1], None, ALU.add))
                    glink(nc.vector.scalar_tensor_tensor(out=ge, in0=gt, scalar=SLOPE, in1=gt,
                                                         op0=ALU.mult, op1=ALU.max))
                    glink(nc.vector.scalar_tensor_tensor(out=gt, in0=gadj, scalar=0.0, in1=ge,
                                                         op0=ALU.is_gt, op1=ALU.mult))
                    glink(nc.vector.tensor_scalar(ge, gadj, 0.0, -1.0, ALU.is_gt, ALU.add))
                    glink(nc.vector.scalar_tensor_tensor(out=ge, in0=ge, scalar=-NEG_INF, in1=gt,
                                                         op0=ALU.mult, op1=ALU.add))
                    glink(nc.vector.tensor_reduce(gv[:, 1:2], ge, AX_X, ALU.max))
                    nc.vector.tensor_scalar(gv[:, 2:3], gv[:, 1:2], -1.0, None, ALU.mult).then_inc(gen_masked, 1)
                    for h in range(4):
                        dve.wait_ge(gen_turned, k * 4 + h + 1)
                        nc.vector.tensor_copy(gt[:, h * 1024:(h + 1) * 1024],
                                              pt[:, 0, :].bitcast(F32)).then_inc(gen_copied, 1)
                    dve.wait_ge(gen_summed, k + 1)
                    glink(nc.vector.reciprocal(gv[:, 4:5], gv[:, 3:4]))
                    glink(nc.vector.scalar_tensor_tensor(out=gy[:, 1, :], in0=acc[:, 0, 0:D], scalar=gv[:, 4:5],
                                                         in1=gx, op0=ALU.mult, op1=ALU.add))
                    glink(nc.vector.tensor_reduce(gv[:, 5:6], gy[:, 1, :], AX_X, ALU.add))
                    glink(nc.vector.tensor_scalar(gv[:, 6:7], gv[:, 5:6], -1.0 / D, None, ALU.mult))
                    glink(nc.vector.tensor_scalar(gy[:, 2, :], gy[:, 1, :], gv[:, 6:7], None, ALU.add))
                    glink(nc.vector.tensor_tensor(gy[:, 0, :], gy[:, 2, :], gy[:, 2, :], ALU.mult))
                    glink(nc.vector.tensor_reduce(gv[:, 5:6], gy[:, 0, :], AX_X, ALU.add))
                    nc.vector.tensor_scalar(gv[:, 7:8], gv[:, 5:6], 1.0 / D, EPS, ALU.mult,
                                            ALU.add).then_inc(gen_var, 1)
                    dve.wait_ge(gen_dev, k + 1)
                    glink(nc.vector.reciprocal(gv[:, 9:10], gv[:, 8:9]))
                    nc.vector.tensor_scalar(gy[:, 3, :], gy[:, 2, :], gv[:, 9:10], None, ALU.mult).then_inc(gen_res, 1)
                    assert chain[0] == STEPS

        @block.gpsimd
        def _(pool):
            for square in (ident16h, ident16, ident):
                nc.gpsimd.memset(square[:, :], 0.0).then_inc(zeroed, 1)
            nc.gpsimd.memset(ones[:, :], 1.0).then_inc(consts_ready, 1)
            nc.gpsimd.memset(ratio[:, :, 1], 1.0).then_inc(consts_ready, 1)
            nc.gpsimd.memset(eps[:, :], EPS).then_inc(consts_ready, 1)
            nc.gpsimd.memset(inv_d[:, :], 1.0 / D).then_inc(consts_ready, 1)
            nc.gpsimd.memset(neg_half[:, :], -0.5).then_inc(consts_ready, 1)
            pool.wait_ge(zeroed, 3)
            for square in (ident16h, ident16, ident):
                nc.gpsimd.affine_select(out=square[:, :], in_=square[:, :], compare_op=ALU.not_equal, fill=1.0,
                                        base=0, pattern=[[-1, P]], channel_multiplier=1).then_inc(consts_ready, 1)
            for q in (0, 2):
                pool.wait_ge(x_high, q + 1)
                bs = slice(q * (NB // Q), (q + 1) * (NB // Q))
                nc.gpsimd.tensor_tensor(x16[:, bs, 1, :], xs[:, bs, :], x16[:, bs, 0, :],
                                        ALU.subtract).then_inc(x_low[q], 1)
            pool.wait_ge(x_high, Q)
            half = NB // 2
            nc.gpsimd.tensor_tensor(tree[:, :, :], xs[:, 0:half, :], xs[:, half:NB, :], ALU.add).then_inc(tree_step, 1)
            pool.wait_ge(stats_ready, 1)
            nc.gpsimd.partition_all_reduce(top[:, :], stats[:, :], P, RMAX).then_inc(top_ready, 1)
            steps = 1
            while half > 1:
                half //= 2
                pool.wait_ge(tree_step, steps)
                ins = nc.gpsimd.tensor_tensor(tree[:, 0:half, :], tree[:, 0:half, :], tree[:, half:2 * half, :],
                                              ALU.add)
                ins.then_inc(tree_step if half > 1 else tree_ready, 1)
                steps += 1
            for half, w in ((0, 0), (0, 1), (1, 0)):
                if half == 1:
                    pool.wait_ge(g32_ready[0], 2)
                    nc.gpsimd.tensor_tensor(g32[:, 1, HALF:NB, 0:D], xs[:, HALF:NB, :],
                                            e12[:, 1, HALF:NB].unsqueeze(2).to_broadcast([P, HALF, D]),
                                            ALU.mult).then_inc(g32_by_pool, 1)
                pool.wait_ge(ghi_ready[half], w + 1)
                bs = slice(half * HALF, (half + 1) * HALF)
                nc.gpsimd.tensor_tensor(g[:, w, bs, 1, :], g32[:, w, bs, :], g[:, w, bs, 0, :],
                                        ALU.subtract).then_inc(glo_ready[half], 1)
            pool.wait_ge(mean_ready, 1)

            def deviation(c, link):
                pool.wait_ge(vsum_ready, c + 1)
                link(nc.gpsimd.tensor_tensor(vmean[:, :], vsum[:, :], inv_d[:, :], ALU.mult))
                link(nc.gpsimd.tensor_tensor(var[:, :], vmean[:, :], eps[:, :], ALU.add))
                nc.gpsimd.tensor_tensor(rstd[:, :], var[:, :], neg_half[:, :], ALU.pow).then_inc(rstd_ready, 1)
                pool.wait_ge(rstd_ready, c + 1)

            ROWS_STEPS = 9

            def rows_out(c, link):
                pool.wait_ge(rden_ready, c + 1)
                link(nc.gpsimd.tensor_tensor(fill[:, :, :], mean_row[:, :].unsqueeze(1).to_broadcast([P, T, D]),
                                             empty[:, :].unsqueeze(2).to_broadcast([P, T, D]), ALU.mult))
                link(nc.gpsimd.tensor_tensor(att[:, :, :], total[:, :, 0:D],
                                             rden[:, :].unsqueeze(2).to_broadcast([P, T, D]), ALU.mult))
                link(nc.gpsimd.tensor_tensor(full[:, :, :], att[:, :, :], fill[:, :, :], ALU.add))
                rows = slice(c * T, (c + 1) * T) if isinstance(c, int) else bass.ds(c * T, T)
                nc.gpsimd.tensor_tensor(z[:, :, :], full[:, :, :], xs[:, rows, :], ALU.add).then_inc(z_ready, 1)

            def centre(c, link):
                pool.wait_ge(zsum_ready, c + 1)
                link(nc.gpsimd.tensor_tensor(mean[:, :], zsum[:, :], inv_d[:, :], ALU.mult))
                link(nc.gpsimd.tensor_tensor(zc[:, :, :], z[:, :, :],
                                             mean[:, :].unsqueeze(2).to_broadcast([P, T, D]), ALU.subtract))
                nc.gpsimd.tensor_tensor(sq[:, :, :], zc[:, :, :], zc[:, :, :], ALU.mult).then_inc(sq_ready, 1)

            def chunk(c, first=False):
                chain = [0]

                def link(ins):
                    chain[0] += 1
                    ins.then_inc(rows_step, 1)
                    pool.wait_ge(rows_step, c * ROWS_STEPS + chain[0])

                pool.wait_ge(sums_taken, c * T + 2 * T)
                link(nc.gpsimd.tensor_tensor(both[:, :, 0, :], both[:, :, 0, :], both[:, :, 1, :], ALU.add))
                nc.gpsimd.tensor_tensor(total[:, :, :], both[:, :, 0, 0:W], both[:, :, 0, W:2 * W],
                                        ALU.add).then_inc(total_ready, 1)
                rows_out(c, link)
                centre(c, link)
                deviation(c, link)
                if not first:
                    pool.wait_ge(res_stored, c * 16)
                link(nc.gpsimd.tensor_tensor(res[:, :, :], zc[:, :, :],
                                             rstd[:, :].unsqueeze(2).to_broadcast([P, T, D]), ALU.mult))
                pool.dma_start(out_b[:, bass.ds(c * (T // 2), T // 2)], pairs(res)).then_inc(res_stored, 16)
                assert chain[0] == ROWS_STEPS

            chunk(0, first=True)
            with pool.Fori(1, C - 1) as c:
                chunk(c)
            for k, tiles in enumerate((EARLY, [T - 1])):
                pool.wait_ge(last_var_ready, tiles[-1] + 1)
                ts = slice(tiles[0], tiles[-1] + 1)
                nc.gpsimd.tensor_tensor(last_rstd[:, ts], last_var[:, ts], neg_half[:, ts],
                                        ALU.pow).then_inc(last_rstd_ready, 1)
            pool.wait_ge(res_stored, (C - 1) * 16)


def kernel(x, adj, L0_gnn_a):
    import numpy as _np
    import concourse.bacc as _bacc
    from concourse import mybir as _mybir
    from concourse.bass_utils import run_bass_kernel_spmd as _run

    nc = _bacc.Bacc("TRN2", target_bir_lowering=False, num_devices=1)
    arrays, args = {}, []
    for name, value in (("x", x), ("adj", adj), ("a", L0_gnn_a)):
        value = _np.ascontiguousarray(value)
        arrays[f"in_{name}"] = value
        args.append(nc.dram_tensor(f"in_{name}", value.shape, _mybir.dt.from_np(value.dtype),
                                   kind="ExternalInput").ap())
    out = nc.dram_tensor("out_0", tuple(x.shape), _mybir.dt.float32, kind="ExternalOutput").ap()
    gat_layernorm(nc, *args, out)
    result = _run(nc, [arrays], core_ids=[0])
    return result.results[0]["out_0"]
```
